# Optimizing a Trainium2 kernel written in Bass

```python
import numpy as np
import jax
import jax.numpy as jnp

def _softmax(x, axis=-1):
    return jax.nn.softmax(x, axis=axis)

def _gelu(x):
    return jax.nn.gelu(x, approximate=True)

def _silu(x):
    return jax.nn.silu(x)

def _sigmoid(x):
    return jax.nn.sigmoid(x)

def _layernorm(x, axis=-1, eps=1e-05):
    m = jnp.mean(x, axis=axis, keepdims=True)
    v = jnp.var(x, axis=axis, keepdims=True)
    return (x - m) / jnp.sqrt(v + eps)

def _scatter_add(tgt, idx, src, axis=0):
    return tgt.at[idx].add(src)

def _segment_sum(src, seg, n):
    return jax.ops.segment_sum(src, seg, n)
kernel_name = 'mk_flamingo_gated_d2_seqx_r4_7acba7'

def setup_inputs(seed: int=0):
    np.random.seed(seed)
    _w = jnp.asarray

    def _rec_inputs():
        import jax
        import jax.numpy as jnp
        _rk = jax.random.key(seed)
        x = 7.22e-05 + 1 * jax.random.normal(jax.random.fold_in(_rk, 1), (32, 256, 256), jnp.float32)
        _lenS = 256 - jax.random.randint(jax.random.fold_in(_rk, 7), (32,), 0, max(1, 256 // 4) + 1, jnp.int32)
        _lenS2 = 256 - jax.random.randint(jax.random.fold_in(_rk, 8), (32,), 0, max(1, 256 // 4) + 1, jnp.int32)
        _ctx_1024P = jax.random.normal(jax.random.fold_in(_rk, 11), (32, 16, 256), jnp.float32)
        _ctx_1024c = jax.random.dirichlet(jax.random.fold_in(_rk, 511), 0.3 * jnp.ones((16,), jnp.float32), (32, 256))
        _ctx_1024t = jnp.einsum('bsk,bkd->bsd', _ctx_1024c, _ctx_1024P)
        _ctx_1024t = _ctx_1024t * jax.lax.rsqrt(jnp.mean(jnp.square(_ctx_1024t)) + 1e-12) * 0.953939
        ctx_1024 = 4.13588e-05 + 0.999923 * (_ctx_1024t + 0.3 * jax.random.normal(jax.random.fold_in(_rk, 611), (32, 256, 256), jnp.float32))
        _g = jax.random.normal(jax.random.fold_in(_rk, 9001), (2, 2), jnp.float32)
        _g = jnp.sign(_g) * jnp.maximum(jnp.abs(_g), 1.0) + (_g == 0) * 1.0
        g_xattn = _g[0]
        g_ffn = _g[1]
        return (x, ctx_1024, g_xattn, g_ffn)
    x, ctx_1024, g_xattn, g_ffn = _rec_inputs()

    def _L0_xattn_setup():
        import jax, jax.numpy as jnp
        import numpy as np
        EMB_DIM = 256
        NUM_HEADS = 16
        HEAD_DIM = EMB_DIM // NUM_HEADS
        key = jax.random.key(seed)
        ks = jax.random.split(key, 7)
        B, S, E = (4, 512, EMB_DIM)
        scale = 1.0 / np.sqrt(E)
        return {'q': jax.random.normal(ks[0], (B, S, E), dtype=jnp.float32), 'k': jax.random.normal(ks[1], (B, S, E), dtype=jnp.float32), 'v': jax.random.normal(ks[2], (B, S, E), dtype=jnp.float32), 'Wq': jax.random.normal(ks[3], (E, E), dtype=jnp.float32) * scale, 'Wk': jax.random.normal(ks[4], (E, E), dtype=jnp.float32) * scale, 'Wv': jax.random.normal(ks[5], (E, E), dtype=jnp.float32) * scale, 'Wo': jax.random.normal(ks[6], (E, E), dtype=jnp.float32) * scale}
    _L0_xattn_all = _L0_xattn_setup()
    _L0_xattn_in = {k: v for k, v in _L0_xattn_all.items() if k in ('Wq', 'Wk', 'Wv', 'Wo')}
    del _L0_xattn_all

    def _L0_ffn_setup():
        import jax, jax.numpy as jnp
        import numpy as np
        EPS = 1e-08

        def _ternary_linear(x, w):
            alpha = jnp.mean(jnp.abs(w))
            w_t = jnp.sign(w) * (jnp.abs(w) > 0.5 * alpha).astype(w.dtype)
            w_q = w + jax.lax.stop_gradient(w_t - w)
            d = x.shape[-1]
            rms = jnp.sqrt(jnp.sum(x * x, axis=-1, keepdims=True)) / jnp.sqrt(jnp.asarray(d, x.dtype))
            x_norm = x / (rms + EPS)
            return jnp.einsum('bsd,fd->bsf', x_norm, w_q)
        key = jax.random.key(seed)
        k1, k2, k3 = jax.random.split(key, 3)
        d_model, d_ff = (256, 1024)
        B, S = (4, 1024)
        x = jax.random.normal(k1, (B, S, d_model), dtype=jnp.float32)
        w_up = jax.random.normal(k2, (d_ff, d_model), dtype=jnp.float32) * 0.02
        w_down = jax.random.normal(k3, (d_model, d_ff), dtype=jnp.float32) * 0.02
        return {'x': x, 'w_up': w_up, 'w_down': w_down}
    _L0_ffn_all = _L0_ffn_setup()
    _L0_ffn_in = {k: v for k, v in _L0_ffn_all.items() if k in ('w_up', 'w_down')}
    del _L0_ffn_all

    def _L1_xattn_setup():
        import jax, jax.numpy as jnp
        import numpy as np
        D_MODEL = 256
        N_HEADS = 16
        HEAD_DIM = D_MODEL // N_HEADS
        SCALE = HEAD_DIM ** (-0.5)
        key = jax.random.key(seed)
        ks = jax.random.split(key, 11)
        B, L = (4, 512)
        s = 1.0 / np.sqrt(D_MODEL)
        inp = {'queries': jax.random.normal(ks[0], (B, L, D_MODEL), jnp.float32), 'keys': jax.random.normal(ks[1], (B, L, D_MODEL), jnp.float32), 'values': jax.random.normal(ks[2], (B, L, D_MODEL), jnp.float32), 'Wq': jax.random.normal(ks[3], (D_MODEL, D_MODEL), jnp.float32) * s, 'bq': jnp.zeros((D_MODEL,), jnp.float32), 'Wk': jax.random.normal(ks[4], (D_MODEL, D_MODEL), jnp.float32) * s, 'bk': jnp.zeros((D_MODEL,), jnp.float32), 'Wv': jax.random.normal(ks[5], (D_MODEL, D_MODEL), jnp.float32) * s, 'bv': jnp.zeros((D_MODEL,), jnp.float32), 'Wo': jax.random.normal(ks[6], (D_MODEL, D_MODEL), jnp.float32) * s, 'bo': jnp.zeros((D_MODEL,), jnp.float32)}
        return inp
    _L1_xattn_all = _L1_xattn_setup()
    _L1_xattn_in = {k: v for k, v in _L1_xattn_all.items() if k in ('Wq', 'bq', 'Wk', 'bk', 'Wv', 'bv', 'Wo', 'bo')}
    del _L1_xattn_all

    def _L1_ffn_setup():
        import jax, jax.numpy as jnp
        import numpy as np
        TOP_K = 2

        def _gelu(x):
            return jax.nn.gelu(x, approximate=False)
        key = jax.random.key(seed)
        ks = jax.random.split(key, 6)
        B, S, D, F, E = (2, 512, 256, 512, 8)
        sc_g = 1.0 / np.sqrt(D)

        def xav(k, shape, fan_in, fan_out):
            lim = np.sqrt(6.0 / (fan_in + fan_out))
            return jax.random.uniform(k, shape, jnp.float32, -lim, lim)
        return {'x': jax.random.normal(ks[0], (B, S, D), jnp.float32), 'Wg': xav(ks[1], (D, E), D, E), 'Wu': xav(ks[2], (E, D, F), D, F), 'Wd': xav(ks[3], (E, F, D), F, D), 'W1': xav(ks[4], (D, F), D, F), 'W2': xav(ks[5], (F, D), F, D)}
    _L1_ffn_all = _L1_ffn_setup()
    _L1_ffn_in = {k: v for k, v in _L1_ffn_all.items() if k in ('Wg', 'Wu', 'Wd', 'W1', 'W2')}
    del _L1_ffn_all
    return {'x': x, 'ctx_1024': ctx_1024, 'g_xattn': g_xattn, 'g_ffn': g_ffn, 'L0_xattn_Wq': _L0_xattn_in['Wq'], 'L0_xattn_Wk': _L0_xattn_in['Wk'], 'L0_xattn_Wv': _L0_xattn_in['Wv'], 'L0_xattn_Wo': _L0_xattn_in['Wo'], 'L0_ffn_w_up': _L0_ffn_in['w_up'], 'L0_ffn_w_down': _L0_ffn_in['w_down'], 'L1_xattn_Wq': _L1_xattn_in['Wq'], 'L1_xattn_bq': _L1_xattn_in['bq'], 'L1_xattn_Wk': _L1_xattn_in['Wk'], 'L1_xattn_bk': _L1_xattn_in['bk'], 'L1_xattn_Wv': _L1_xattn_in['Wv'], 'L1_xattn_bv': _L1_xattn_in['bv'], 'L1_xattn_Wo': _L1_xattn_in['Wo'], 'L1_xattn_bo': _L1_xattn_in['bo'], 'L1_ffn_Wg': _L1_ffn_in['Wg'], 'L1_ffn_Wu': _L1_ffn_in['Wu'], 'L1_ffn_Wd': _L1_ffn_in['Wd'], 'L1_ffn_W1': _L1_ffn_in['W1'], 'L1_ffn_W2': _L1_ffn_in['W2']}

def reference(x, ctx_1024, g_xattn, g_ffn, L0_xattn_Wq, L0_xattn_Wk, L0_xattn_Wv, L0_xattn_Wo, L0_ffn_w_up, L0_ffn_w_down, L1_xattn_Wq, L1_xattn_bq, L1_xattn_Wk, L1_xattn_bk, L1_xattn_Wv, L1_xattn_bv, L1_xattn_Wo, L1_xattn_bo, L1_ffn_Wg, L1_ffn_Wu, L1_ffn_Wd, L1_ffn_W1, L1_ffn_W2):
    import jax
    import jax.numpy as jnp

    def _L0_xattn_ref(q, k, v, Wq, Wk, Wv, Wo):
        import jax, jax.numpy as jnp
        import numpy as np
        EMB_DIM = 256
        NUM_HEADS = 16
        HEAD_DIM = EMB_DIM // NUM_HEADS
        B, S, E = q.shape
        H, D = (NUM_HEADS, HEAD_DIM)
        qh = (q @ Wq.T).reshape(B, S, H, D).transpose(0, 2, 1, 3)
        kh = (k @ Wk.T).reshape(B, S, H, D).transpose(0, 2, 1, 3)
        vh = (v @ Wv.T).reshape(B, S, H, D).transpose(0, 2, 1, 3)
        scores = jnp.einsum('bhse,bhte->bhst', qh, kh) / jnp.sqrt(jnp.float32(D))
        attn = jax.nn.softmax(scores, axis=-1)
        out = jnp.einsum('bhst,bhtd->bshd', attn, vh).reshape(B, S, E)
        return out @ Wo.T

    def _L0_ffn_ref(x, w_up, w_down):
        import jax, jax.numpy as jnp
        import numpy as np
        EPS = 1e-08

        def _ternary_linear(x, w):
            alpha = jnp.mean(jnp.abs(w))
            w_t = jnp.sign(w) * (jnp.abs(w) > 0.5 * alpha).astype(w.dtype)
            w_q = w + jax.lax.stop_gradient(w_t - w)
            d = x.shape[-1]
            rms = jnp.sqrt(jnp.sum(x * x, axis=-1, keepdims=True)) / jnp.sqrt(jnp.asarray(d, x.dtype))
            x_norm = x / (rms + EPS)
            return jnp.einsum('bsd,fd->bsf', x_norm, w_q)
        h = jax.nn.gelu(_ternary_linear(x, w_up), approximate=False)
        return _ternary_linear(h, w_down)

    def _L1_xattn_ref(queries, keys, values, Wq, bq, Wk, bk, Wv, bv, Wo, bo):
        import jax, jax.numpy as jnp
        import numpy as np
        D_MODEL = 256
        N_HEADS = 16
        HEAD_DIM = D_MODEL // N_HEADS
        SCALE = HEAD_DIM ** (-0.5)
        B, L, _ = queries.shape
        S = keys.shape[1]
        q = (queries @ Wq + bq).reshape(B, L, N_HEADS, HEAD_DIM).transpose(0, 2, 1, 3)
        k = (keys @ Wk + bk).reshape(B, S, N_HEADS, HEAD_DIM).transpose(0, 2, 1, 3)
        v = (values @ Wv + bv).reshape(B, S, N_HEADS, HEAD_DIM).transpose(0, 2, 1, 3)
        scores = jnp.einsum('bhld,bhsd->bhls', q, k) * SCALE
        weights = jax.nn.softmax(scores, axis=-1)
        out = jnp.einsum('bhls,bhsd->bhld', weights, v)
        out = out.transpose(0, 2, 1, 3).reshape(B, L, D_MODEL)
        out = out @ Wo + bo
        return out

    def _L1_ffn_ref(x, Wg, Wu, Wd, W1, W2):
        import jax, jax.numpy as jnp
        import numpy as np
        TOP_K = 2

        def _gelu(x):
            return jax.nn.gelu(x, approximate=False)
        B, S, D = x.shape
        E = Wu.shape[0]
        T = B * S
        xt = x.reshape(T, D)
        probs = jax.nn.softmax(xt @ Wg, axis=-1)
        topv, topi = jax.lax.top_k(probs, TOP_K)
        topv = topv / jnp.sum(topv, axis=-1, keepdims=True)
        cw = jnp.zeros((T, E), x.dtype).at[jnp.arange(T)[:, None], topi].set(topv)
        h = _gelu(jnp.einsum('td,edf->tef', xt, Wu))
        y = jnp.einsum('tef,efd->ted', h, Wd)
        moe = jnp.einsum('ted,te->td', y, cw)
        shared = _gelu(xt @ W1) @ W2
        return (shared + moe).reshape(B, S, D)
    x = x + jnp.tanh(g_xattn[0]) * _L0_xattn_ref(_layernorm(x, axis=-1), ctx_1024, ctx_1024, L0_xattn_Wq, L0_xattn_Wk, L0_xattn_Wv, L0_xattn_Wo)
    x = x + jnp.tanh(g_ffn[0]) * _L0_ffn_ref(_layernorm(x, axis=-1), L0_ffn_w_up, L0_ffn_w_down)
    x = x + jnp.tanh(g_xattn[1]) * _L1_xattn_ref(_layernorm(x, axis=-1), ctx_1024, ctx_1024, L1_xattn_Wq, L1_xattn_bq, L1_xattn_Wk, L1_xattn_bk, L1_xattn_Wv, L1_xattn_bv, L1_xattn_Wo, L1_xattn_bo)
    x = x + jnp.tanh(g_ffn[1]) * _L1_ffn_ref(_layernorm(x, axis=-1), L1_ffn_Wg, L1_ffn_Wu, L1_ffn_Wd, L1_ffn_W1, L1_ffn_W2)
    return x

_drawn_inputs = setup_inputs


def setup_inputs(seed=0):
    import zlib

    import numpy as np

    out = dict(_drawn_inputs(seed))
    spreads = {'g_ffn': (-1.0, 0.6),
     'L1_xattn_bq': (0.0, 0.8),
     'L1_xattn_bk': (0.0, 0.8),
     'L1_xattn_bv': (0.0, 0.8),
     'L1_xattn_bo': (0.0, 0.8)}
    factors = {'L1_xattn_Wq': 5.797,
     'L1_xattn_Wk': 5.804,
     'L1_ffn_Wg': 3.326,
     'L1_ffn_Wu': 3.262,
     'L1_ffn_Wd': 2.949}
    for name, (base, spread) in spreads.items():
        noise = np.random.default_rng([zlib.crc32(name.encode()), seed]).standard_normal(out[name].shape)
        drawn = base * np.exp(spread * noise) if base else spread * noise
        out[name] = jnp.asarray(drawn.astype(out[name].dtype))
    for name, factor in factors.items():
        out[name] = (out[name] * factor).astype(out[name].dtype)
    return out
```

```python
from contextlib import ExitStack

import numpy as np

import concourse.bass as bass
from concourse import mybir

F32 = mybir.dt.float32
F16 = mybir.dt.float16
I32 = mybir.dt.int32
U32 = mybir.dt.uint32
ACT = mybir.ActivationFunctionType
ALU = mybir.AluOpType
AX_X = mybir.AxisListType.X

P = 128
D = 256
DC = D // P
S = 256
TT = S // P
H = 16
DH = D // H
G = 4
NG = H // G
HI, LO = 0, 1
WS = 16.0
MS = 64.0
EPS = 1e-5
PASSES = ((HI, HI), (LO, HI), (HI, LO))


def clear(nc, sems):
    with nc.Block() as block:
        @block.gpsimd
        def _(pool):
            for s in sems:
                pool.sem_clear(s)


class At:

    def __init__(self, it, c):
        self.it, self.c = it, c

    def __add__(self, n):
        return At(self.it, self.c + n)

    def __sub__(self, n):
        return At(self.it, self.c - n)

    def par(self):
        return self.c % 2

    def index(self):
        return self.c if self.it is None else self.it * 2 + self.c

    def count(self, per, k):
        v = per * self.c + k
        return v if self.it is None else self.it * (2 * per) + v

    def half(self, per, k):
        v = per * (self.c // 2) + k
        return v if self.it is None else self.it * per + v


def wait(eng, sem, value, alone=None):
    if isinstance(value, int) and value <= 0:
        return
    eng.wait_ge(sem, value)
    if alone is not None and not isinstance(value, int):
        eng.sem_inc(alone, 1)


def split_weight(dve, sem, n, w32, w16, scale):
    dve.tensor_scalar(w32, w32, scale, None, ALU.mult).then_inc(sem, 1)
    dve.wait_ge(sem, n + 1)
    dve.tensor_copy(w16[:, HI], w32).then_inc(sem, 1)
    dve.wait_ge(sem, n + 2)
    dve.tensor_tensor(w16[:, LO], w32, w16[:, HI], ALU.subtract).then_inc(sem, 1)
    return n + 3


def attention(nc, tag, NB, x_in, ctxT, wqT, wkT, wvT, woT, bias, gate, x_out):
    x_b = x_in.rearrange("(b t p) d -> b p t d", t=TT, p=P)
    o_b = x_out.rearrange("(b t p) d -> b p t d", t=TT, p=P)
    c_b = ctxT.rearrange("(k p) (b s) -> b p k s", p=P, s=S)
    pack_q = nc.dram_tensor(f"{tag}_pack_q", (2, 2, DH, H, S), F16, kind="Internal").ap()
    pack_k = nc.dram_tensor(f"{tag}_pack_k", (2, 2, DH, H, S), F16, kind="Internal").ap()
    HH = H // 2

    sems = []
    with ExitStack() as ctx:
        def sb(name, shape, dt):
            return ctx.enter_context(nc.sbuf_tensor(f"{tag}_{name}", shape, dt))

        def pb(name, shape, dt):
            return ctx.enter_context(nc.psum_tensor(f"{tag}_{name}", shape, dt))

        def sem(name):
            sems.append(ctx.enter_context(nc.semaphore(f"{tag}_{name}")))
            return sems[-1]

        wq16 = sb("wq16", [P, 2, DC, D], F16)
        wk16 = sb("wk16", [P, 2, DC, D], F16)
        wv16 = sb("wv16", [P, 2, DC, D], F16)
        wo16 = sb("wo16", [P, 2, DC, D], F16)
        wq32 = sb("wq32", [P, DC, D], F32)
        wk32 = sb("wk32", [P, DC, D], F32)
        wv32 = sb("wv32", [P, DC, D], F32)
        wo32 = sb("wo32", [P, DC, D], F32)
        ident = sb("ident", [P, P], F32)
        half_neg = sb("half_neg", [P, TT], F32)
        tg = sb("tg", [P, 1], F32)
        if bias:
            bqk = sb("bqk", [P, 2, DC], F32)
            bv32 = sb("bv32", [1, D], F32)
            bv16 = sb("bv16", [1, 2, D], F16)
            ones16 = sb("ones16", [1, P], F16)
            bo = sb("bo", [P, D], F32)
        xin = sb("xin", [P, 2, TT, D], F32)
        cin = sb("cin", [P, 2, DC, S], F32)
        xres = sb("xres", [P, 2, TT, D], F32)
        bns = sb("bns", [P, TT, 6], F32)
        mv = sb("mv", [P, TT, 2], F32)
        vpe = sb("vpe", [P, TT], F32)
        rstd = sb("rstd", [P, TT], F32)
        xn = sb("xn", [P, TT, D], F32)
        xT = sb("xT", [P, 2, DC, S], F16)
        cT = sb("cT", [P, 2, 2, DC, S], F16)
        qT = sb("qT", [P, 2, DC, S], F16)
        kT = sb("kT", [P, 2, DC, S], F16)
        Qp = sb("Qp", [P, 2, H, S], F16)
        Kp = sb("Kp", [P, 2, H, S], F16)
        Qm = sb("Qm", [P, 2, H, S], F16)
        V = sb("V", [P, 2, TT, H, 32], F32)
        mx = sb("mx", [P, 2, TT, H], F32)
        mrow = sb("mrow", [H, 2, S], F16)
        pr = sb("pr", [P, 2 * G, TT, S], F32)
        ou = sb("ou", [P, NG, S], F32)
        rinv = sb("rinv", [P, 2, 2 * H // 2], F32)
        on = sb("on", [P, TT, D], F32)
        oT = sb("oT", [P, 2, DC, S], F16)

        mx_ps = [pb(f"mx_ps{i}", [P, TT, S], F32) for i in range(2)]
        st_ps = [pb(f"st_ps{i}", [P, TT, S], F32) for i in range(2)]
        pv_ps = [pb(f"pv_ps{i}", [P, 2 * S], F32) for i in range(2)]
        ms_ps = [pb(f"ms_ps{i}", [P, TT, S], F32) for i in range(2)]

        alone = sem("alone")
        l_w = sem("l_w")
        l_wo = sem("l_wo")
        c_pool = sem("c_pool")
        c_tanh = sem("c_tanh")
        c_dve = sem("c_dve")
        l_x = [sem(f"l_x{i}") for i in range(2)]
        l_c = [sem(f"l_c{i}") for i in range(2)]
        l_r = [sem(f"l_r{i}") for i in range(2)]
        st_o = [sem(f"st_o{i}") for i in range(2)]
        d_pack = [sem(f"d_pack{i}") for i in range(2)]
        d_a = [sem(f"d_a{i}") for i in range(2)]
        d_b = [sem(f"d_b{i}") for i in range(2)]
        d_m = [sem(f"d_m{i}") for i in range(2)]
        s_bn = sem("s_bn")
        s_rstd = sem("s_rstd")
        s_xn = sem("s_xn")
        s_xt = sem("s_xt")
        s_xhi = sem("s_xhi")
        s_xlo = sem("s_xlo")
        s_ct = sem("s_ct")
        s_q = sem("s_q")
        s_qhi = sem("s_qhi")
        s_qlo = sem("s_qlo")
        s_k = sem("s_k")
        s_khi = sem("s_khi")
        s_klo = sem("s_klo")
        s_v = sem("s_v")
        s_vev = sem("s_vev")
        s_mm = sem("s_mm")
        s_max = sem("s_max")
        s_mt = sem("s_mt")
        s_mrow = sem("s_mrow")
        s_st = sem("s_st")
        s_exp = sem("s_exp")
        s_pv = sem("s_pv")
        s_ou = sem("s_ou")
        s_at = sem("s_at")
        s_rinv = sem("s_rinv")
        s_on = sem("s_on")
        s_bt = sem("s_bt")
        s_ohi = sem("s_ohi")
        s_olo = sem("s_olo")
        s_o = sem("s_o")
        s_bo = sem("s_bo")
        s_res = sem("s_res")

        BODIES = range(-3, NB + 1)
        LOOP = (3, NB - 3)

        def bodies(eng, body):
            for c in range(BODIES[0], LOOP[0]):
                body(At(None, c), lambda n, c=c: 0 <= c + n < NB)
            with eng.Fori(0, (LOOP[1] - LOOP[0]) // 2) as it:
                for u in range(2):
                    body(At(it, LOOP[0] + u), lambda n: True)
            for c in range(LOOP[1], NB + 1):
                body(At(None, c), lambda n, c=c: 0 <= c + n < NB)

        def max_slots(s):
            return [h for h in range(H) if h * 3 // 4 == s]

        with nc.Block() as block:

            @block.sync
            def _(sp):
                for w32, w in ((wq32, wqT), (wk32, wkT), (wv32, wvT), (wo32, woT)):
                    sp.dma_start(w32[:, :, :], w.rearrange("(k p) n -> p k n", p=P)).then_inc(l_w, 16)
                if bias:
                    for n in range(2):
                        sp.dma_start(bqk[:, n, :], bias[n]).then_inc(l_wo, 16)
                    sp.dma_start(bv32[:, :], bias[2].rearrange("(a n) -> a n", a=1)).then_inc(l_wo, 16)
                    sp.dma_start(bo[:, :], bias[3].rearrange("(a n) -> a n", a=1).broadcast_to([P, D])).then_inc(l_wo, 16)
                sp.dma_start(tg[:, :], gate.rearrange("(a n) -> a n", a=1).broadcast_to([P, 1])).then_inc(l_wo, 16)

                def load_x(b):
                    wait(sp, s_xn, (b - 2).count(TT, TT), alone)
                    sp.dma_start(xin[:, b.par()], x_b[b.index()]).then_inc(l_x[b.par()], 16)

                def load_c(b):
                    wait(sp, s_ct, (b - 2).count(2, 2), alone)
                    sp.dma_start(cin[:, b.par()], c_b[b.index()]).then_inc(l_c[b.par()], 16)

                def pack(b, half):
                    p, h0 = b.par(), half * HH
                    hs = slice(h0, h0 + HH)
                    done = (d_a, d_b)[half][p]
                    for r, (pq, pk) in enumerate(((HI, HI), (HI, LO), (LO, HI), (LO, LO))):
                        rows = slice(DH * r, DH * r + DH)
                        sp.dma_start(Qp[rows, p, hs, :], pack_q[p, pq, :, hs, :]).then_inc(done, 16)
                        sp.dma_start(Kp[rows, p, hs, :], pack_k[p, pk, :, hs, :]).then_inc(done, 16)
                    sp.dma_start(Qm[0:DH, p, hs, :], pack_q[p, HI, :, hs, :]).then_inc(done, 16)

                def body(i, has):
                    if has(3):
                        load_x(i + 3)
                        load_c(i + 3)
                    if has(0):
                        b = i
                        wait(sp, st_o[b.par()], (b - 2).half(16, 16), alone)
                        sp.dma_start(xres[:, b.par()], x_b[b.index()]).then_inc(l_r[b.par()], 16)
                    if has(2):
                        b = i + 2
                        wait(sp, d_a[b.par()], (b - 2).half(144, 144), alone)
                        wait(sp, d_b[b.par()], (b - 2).half(144, 144), alone)
                        for t16, hi, lo, dram in ((qT, s_qhi, s_qlo, pack_q), (kT, s_khi, s_klo, pack_k)):
                            wait(sp, hi, b.count(1, 1), alone)
                            wait(sp, lo, b.count(1, 1), alone)
                            for part in range(2):
                                for t in range(DC):
                                    sp.dma_start(
                                        dram[b.par(), part, :, t * HH:(t + 1) * HH, :].rearrange("d h s -> h d s"),
                                        t16[:, part, t, :]).then_inc(d_pack[b.par()], 16)
                    if has(-1):
                        b = i - 1
                        wait(sp, s_res, b.count(TT, TT), alone)
                        sp.dma_start(o_b[b.index()], xres[:, b.par()]).then_inc(st_o[b.par()], 16)
                    if has(2):
                        b = i + 2
                        wait(sp, d_pack[b.par()], b.half(128, 128), alone)
                        wait(sp, s_mm, i.count(H, H), alone)
                        wait(sp, s_st, i.count(H, HH), alone)
                        if not has(0):
                            sp.wait_ge(c_pool, 6)
                        pack(b, 0)
                    if has(1):
                        b = i + 1
                        wait(sp, s_mrow, b.count(1, 1), alone)
                        sp.dma_start(Qp[64:65, b.par()], mrow[:, b.par(), :]).then_inc(d_m[b.par()], 16)
                    if has(2):
                        wait(sp, s_st, i.count(H, H), alone)
                        pack(i + 2, 1)

                bodies(sp, body)
                for p in range(2):
                    sp.wait_ge(st_o[p], 16 * (NB // 2))

            @block.gpsimd
            def _(pool):
                pool.memset(Qp[:, :, :, :], 0.0).then_inc(c_pool, 1)
                pool.memset(Kp[:, :, :, :], 0.0).then_inc(c_pool, 1)
                pool.memset(Qm[:, :, :, :], 0.0).then_inc(c_pool, 1)
                pool.memset(V[:, :, :, :, :], WS).then_inc(c_pool, 1)
                pool.memset(ident[:, :], 0.0).then_inc(c_pool, 1)
                pool.wait_ge(c_pool, 5)
                pool.memset(Kp[64:65, :, :, :], MS).then_inc(c_pool, 1)
                pool.wait_ge(c_pool, 6)
                pool.affine_select(out=ident[:, :], in_=ident[:, :], compare_op=ALU.not_equal, fill=1.0,
                                   base=0, pattern=[[-1, P]], channel_multiplier=1).then_inc(c_pool, 1)
                pool.memset(half_neg[:, :], -0.5).then_inc(c_pool, 1)
                if bias:
                    pool.memset(ones16[:, :], 1.0).then_inc(c_pool, 1)
                    pool.wait_ge(c_pool, 9)
                pool.wait_ge(c_pool, 8)

                def body(i, has):
                    if has(2):
                        b = i + 2
                        p = b.par()
                        wait(pool, l_c[p], b.half(16, 16), alone)
                        wait(pool, s_v, (b - 2).count(1, 1), alone)
                        pool.tensor_copy(cT[:, p, HI], cin[:, p]).then_inc(s_ct, 1)
                        wait(pool, s_ct, b.count(2, 1), alone)
                        pool.tensor_tensor(cT[:, p, LO], cin[:, p], cT[:, p, HI], ALU.subtract).then_inc(s_ct, 1)

                    if has(-1) and bias:
                        b = i - 1
                        wait(pool, l_r[b.par()], b.half(16, 16), alone)
                        for t in range(TT):
                            pool.tensor_tensor(xres[:, b.par(), t], xres[:, b.par(), t], bo[:, :],
                                               ALU.add).then_inc(s_bo, 1)
                    if has(3):
                        b = i + 3
                        wait(pool, s_bn, b.count(2 * TT, 2 * TT), alone)
                        wait(pool, s_xn, (b - 1).count(TT, TT), alone)
                        pool.tensor_scalar(vpe[:, :], mv[:, :, 1], EPS, None, ALU.add).then_inc(s_rstd, 1)
                        wait(pool, s_rstd, b.count(2, 1), alone)
                        pool.tensor_tensor(rstd[:, :], vpe[:, :], half_neg[:, :], ALU.pow).then_inc(s_rstd, 1)

                bodies(pool, body)

            @block.scalar
            def _(act):
                n_l = 16 * (1 + (4 if bias else 0))
                act.wait_ge(l_wo, n_l)
                act.activation(tg[:, :], tg[:, :], ACT.Tanh).then_inc(c_tanh, 1)
                act.wait_ge(c_dve, 12)
                if bias:
                    act.wait_ge(c_dve, 17)
                act.wait_ge(c_pool, 8)

                def body(i, has):
                    def exp_head(s):
                        b = i
                        wait(act, s_st, b.count(H, s + 1))
                        g = s // G
                        if s % G == 0:
                            wait(act, s_pv, b.count(NG, g - 1))
                        act.activation(pr[:, s % (2 * G)], st_ps[s % 2][:, :, :], ACT.Exp,
                                       scale=DH ** -0.5 / (WS * WS)).then_inc(s_exp, 1)

                    def out_raw(n, g):
                        b = i + n
                        wait(act, s_pv, b.count(NG, g + 1))
                        if g % 2 == 0:
                            wait(act, s_at, (b - 1).count(2, g // 2 + 1))
                        act.activation(ou[:, g, :], pv_ps[g % 2][:, 0:S], ACT.Identity).then_inc(s_ou, 1)

                    def qk_hi(src, dst, there, done, n):
                        b = i + 2
                        wait(act, there, b.count(1, 1))
                        wait(act, d_pack[(b - 1).par()], (b - 1).half(128, 128))
                        if bias:
                            for t in range(DC):
                                ins = act.activation(dst[:, HI, t, :], src[:, t, :], ACT.Identity,
                                                     bias=bqk[:, n, t:t + 1])
                        else:
                            ins = act.activation(dst[:, HI], src[:, :, :], ACT.Identity)
                        ins.then_inc(done, 1)

                    for s in range(H):
                        if has(0):
                            exp_head(s)
                        if s == 0 and has(2):
                            b = i + 2
                            wait(act, s_xt, b.count(1, 1))
                            wait(act, s_q, (b - 1).count(1, 1))
                            act.activation(xT[:, HI], ms_ps[0][:, :, :], ACT.Identity).then_inc(s_xhi, 1)
                        if s == 1 and has(-1):
                            out_raw(-1, 3)
                        if s == 4 and has(-1):
                            b = i - 1
                            wait(act, s_bt, b.count(1, 1))
                            wait(act, s_o, (b - 1).count(1, 1))
                            act.activation(oT[:, HI], ms_ps[0][:, :, :], ACT.Identity).then_inc(s_ohi, 1)
                        if s == 5 and has(2):
                            qk_hi(ms_ps[1], qT, s_q, s_qhi, 0)
                        if s == 8 and has(2):
                            qk_hi(ms_ps[1], kT, s_k, s_khi, 1)
                        if s == 10 and has(1):
                            b = i + 1
                            wait(act, s_v, b.count(1, 1))
                            wait(act, s_pv, (i - 1).count(NG, NG))
                            act.activation(V[:, b.par(), :, :, 0:DH],
                                           ms_ps[0][:, :, :].rearrange("p t (h d) -> p t h d", d=DH),
                                           ACT.Identity).then_inc(s_vev, 1)
                        if s in (7, 11, 15) and has(0):
                            out_raw(0, (s - 7) // 4)
                        if s == 12 and has(1):
                            b = i + 1
                            wait(act, s_mt, b.count(1, 1))
                            wait(act, d_m[b.par()], (b - 2).half(16, 16))
                            act.activation(mrow[:, b.par(), :], ms_ps[1][0:H, 0, :], ACT.Identity,
                                           scale=-1.0 / MS).then_inc(s_mrow, 1)

                bodies(act, body)

            @block.vector
            def _(dve):
                dve.wait_ge(l_w, 64)
                n = 0
                for w32, w16 in ((wq32, wq16), (wk32, wk16), (wv32, wv16)):
                    n = split_weight(dve, c_dve, n, w32[:, :, :], w16, WS)
                dve.wait_ge(l_wo, 16 * (1 + (4 if bias else 0)))
                n = split_weight(dve, c_dve, n, wo32[:, :, :], wo16, WS)
                dve.wait_ge(c_tanh, 1)
                if bias:
                    dve.tensor_scalar(bo[:, :], bo[:, :], tg[:, 0:1], None, ALU.mult).then_inc(c_dve, 1)
                    dve.tensor_scalar(bqk[:, :, :], bqk[:, :, :], WS, None, ALU.mult).then_inc(c_dve, 1)
                    n = split_weight(dve, c_dve, n + 2, bv32[:, :], bv16, WS)
                dve.wait_ge(c_dve, n)
                dve.tensor_scalar(tg[:, :], tg[:, :], 1.0 / WS, None, ALU.mult).then_inc(c_dve, 1)
                dve.wait_ge(c_dve, n + 1)

                def body(i, has):
                    def maxima(h):
                        b = i + 1
                        if h == 0:
                            wait(dve, s_mt, (b - 2).count(1, 1))
                        wait(dve, s_mm, b.count(H, h + 1))
                        dve.tensor_reduce(mx[:, b.par(), :, h], mx_ps[h % 2][:, :, :], AX_X,
                                          ALU.max).then_inc(s_max, 1)

                    def normalise(n, k):
                        b = i + n
                        a = ms_ps[1 if k else 0][:, :, :].rearrange("p t (j e) -> p t j e", e=32)
                        wait(dve, s_at, b.count(2, k + 1))
                        dve.reciprocal(rinv[:, k, :].rearrange("p (t j) -> p t j", t=TT),
                                       a[:, :, :, DH]).then_inc(s_rinv, 1)
                        wait(dve, s_rinv, b.count(2, k + 1))
                        if k == 0:
                            wait(dve, s_bt, (b - 1).count(1, 1))
                        for t in range(TT):
                            ins = dve.tensor_tensor(
                                on[:, t, k * P:(k + 1) * P].rearrange("p (j d) -> p j d", d=DH),
                                a[:, t, :, 0:DH],
                                rinv[:, k, t * HH:(t + 1) * HH].unsqueeze(2).broadcast_to([P, HH, DH]),
                                ALU.mult)
                        ins.then_inc(s_on, 1)

                    def qk_lo(src, dst, hi, done, n):
                        b = i + 2
                        wait(dve, hi, b.count(1, 1))
                        if bias:
                            for t in range(DC):
                                ins = dve.scalar_tensor_tensor(dst[:, LO, t, :], src[:, t, :],
                                                               bqk[:, n, t:t + 1], dst[:, HI, t, :],
                                                               ALU.add, ALU.subtract)
                        else:
                            ins = dve.tensor_tensor(dst[:, LO], src[:, :, :], dst[:, HI], ALU.subtract)
                        ins.then_inc(done, 1)

                    for s in range(H):
                        if has(1):
                            for h in max_slots(s):
                                maxima(h)
                        if s == 0 and has(2):
                            wait(dve, s_xhi, (i + 2).count(1, 1))
                            dve.tensor_tensor(xT[:, LO], ms_ps[0][:, :, :], xT[:, HI],
                                              ALU.subtract).then_inc(s_xlo, 1)
                        if s == 2 and has(-1):
                            normalise(-1, 1)
                        if s == 4 and has(-1):
                            wait(dve, s_ohi, (i - 1).count(1, 1))
                            dve.tensor_tensor(oT[:, LO], ms_ps[0][:, :, :], oT[:, HI],
                                              ALU.subtract).then_inc(s_olo, 1)
                        if s == 5 and has(2):
                            qk_lo(ms_ps[1], qT, s_qhi, s_qlo, 0)
                        if s == 7 and has(-1):
                            b = i - 1
                            wait(dve, s_o, b.count(1, 1))
                            if bias:
                                wait(dve, s_bo, b.count(TT, TT))
                            wait(dve, l_r[b.par()], b.half(16, 16))
                            for t in range(TT):
                                dve.scalar_tensor_tensor(xres[:, b.par(), t], ms_ps[0][:, t, :], tg[:, 0:1],
                                                         xres[:, b.par(), t], ALU.mult, ALU.add).then_inc(s_res, 1)
                        if s == 8 and has(2):
                            qk_lo(ms_ps[1], kT, s_khi, s_klo, 1)
                        if s == 12 and has(3):
                            b = i + 3
                            wait(dve, l_x[b.par()], b.half(16, 16))
                            wait(dve, s_rstd, (b - 1).count(2, 2))
                            for t in range(TT):
                                dve.bn_stats(bns[:, t, :], xin[:, b.par(), t]).then_inc(s_bn, 1)
                            for t in range(TT):
                                wait(dve, s_bn, b.count(2 * TT, t + 1), alone)
                                dve.bn_aggr(mv[:, t, :], bns[:, t, :]).then_inc(s_bn, 1)
                        if s == 13 and has(0):
                            normalise(0, 0)
                        if s == 14 and has(3):
                            b = i + 3
                            wait(dve, s_rstd, b.count(2, 2))
                            wait(dve, s_xt, (b - 1).count(1, 1))
                            for t in range(TT):
                                dve.tensor_scalar(xn[:, t], xin[:, b.par(), t], mv[:, t, 0:1], rstd[:, t:t + 1],
                                                  ALU.subtract, ALU.mult).then_inc(s_xn, 1)

                bodies(dve, body)

            @block.tensor
            def _(pe):
                pe.wait_ge(c_dve, 18 if bias else 13)
                pe.wait_ge(c_pool, 9 if bias else 8)

                def body(i, has):
                    mm = nc.tensor.matmul

                    def scores_max(h):
                        b = i + 1
                        p = b.par()
                        if h % HH == 0:
                            wait(pe, (d_a, d_b)[h // HH][p], b.half(144, 144))
                        wait(pe, s_max, b.count(H, h - 1))
                        for t in range(TT):
                            ins = mm(mx_ps[h % 2][:, t, :], Qm[:, p, h, t * P:(t + 1) * P], Kp[:, p, h, :],
                                     start=True, stop=True)
                        ins.then_inc(s_mm, 1)

                    def scores(s):
                        p = i.par()
                        if s == 0:
                            wait(pe, d_m[p], i.half(16, 16))
                        wait(pe, s_exp, i.count(H, s - 1))
                        for t in range(TT):
                            ins = mm(st_ps[s % 2][:, t, :], Kp[:, p, s, t * P:(t + 1) * P], Qp[:, p, s, :],
                                     start=True, stop=True)
                        ins.then_inc(s_st, 1)

                    def values(g):
                        wait(pe, s_exp, i.count(H, G * g + G))
                        if g == 0:
                            wait(pe, s_vev, i.count(1, 1))
                        wait(pe, s_ou, i.count(NG, g - 1))
                        for t in range(TT):
                            for j in range(G):
                                h = G * g + j
                                ins = mm(pv_ps[g % 2][32 * j:32 * j + 32, 0:S], V[:, i.par(), t, h, :],
                                         pr[:, h % (2 * G), t, :], start=(t == 0), stop=(t == TT - 1),
                                         tile_position=(0, 32 * j))
                        ins.then_inc(s_pv, 1)

                    def out_transposed(n, k):
                        b = i + n
                        wait(pe, s_ou, b.count(NG, 2 * k + 2))
                        for t in range(TT):
                            for g in range(2):
                                ins = pe.transpose(ms_ps[k][:, t, g * P:(g + 1) * P],
                                                   ou[:, 2 * k + g, t * P:(t + 1) * P], ident[:, :])
                        ins.then_inc(s_at, 1)

                    def project(w16, src, dst, done):
                        for m in range(DC):
                            n = 0
                            for k in range(DC):
                                for pw, px in PASSES:
                                    ins = mm(dst[:, m, :], w16[:, pw, k, m * P:(m + 1) * P], src[:, px, k, :],
                                             start=(n == 0), stop=(n == 5))
                                    n += 1
                        ins.then_inc(done, 1)

                    for s in range(H):
                        if s == 0 and has(2):
                            b = i + 2
                            wait(pe, s_xn, b.count(TT, TT))
                            if has(-1):
                                wait(pe, s_on, (i - 1).count(2, 1))
                            elif has(0):
                                wait(pe, s_vev, i.count(1, 1))
                            else:
                                wait(pe, s_xlo, (i + 1).count(1, 1))
                            for k in range(DC):
                                for t in range(TT):
                                    ins = pe.transpose(ms_ps[0][:, k, t * P:(t + 1) * P],
                                                       xn[:, t, k * P:(k + 1) * P], ident[:, :])
                            ins.then_inc(s_xt, 1)
                        if s == 2 and has(-1):
                            if has(0):
                                wait(pe, s_mrow, i.count(1, 1))
                            else:
                                wait(pe, s_on, (i - 2).count(2, 2))
                            out_transposed(-1, 1)
                        if s == 4 and has(-1):
                            b = i - 1
                            wait(pe, s_on, b.count(2, 2))
                            if has(2):
                                wait(pe, s_xlo, (i + 2).count(1, 1))
                            for k in range(DC):
                                for t in range(TT):
                                    ins = pe.transpose(ms_ps[0][:, k, t * P:(t + 1) * P],
                                                       on[:, t, k * P:(k + 1) * P], ident[:, :])
                            ins.then_inc(s_bt, 1)
                        if s == 5 and has(2):
                            b = i + 2
                            wait(pe, s_xlo, b.count(1, 1))
                            if has(-1):
                                wait(pe, s_on, (i - 1).count(2, 2))
                            elif has(0):
                                wait(pe, s_mrow, i.count(1, 1))
                            else:
                                wait(pe, s_klo, (i + 1).count(1, 1))
                            project(wq16, xT, ms_ps[1], s_q)
                        if s == 7 and has(-1):
                            b = i - 1
                            wait(pe, s_olo, b.count(1, 1))
                            for t in range(TT):
                                n = 0
                                for k in range(DC):
                                    for pw, px in PASSES:
                                        ins = mm(ms_ps[0][:, t, :], oT[:, px, k, t * P:(t + 1) * P],
                                                 wo16[:, pw, k, :], start=(n == 0), stop=(n == 5))
                                        n += 1
                            ins.then_inc(s_o, 1)
                        if s == 8 and has(2):
                            b = i + 2
                            wait(pe, s_ct, b.count(2, 2))
                            wait(pe, s_qlo, b.count(1, 1))
                            project(wk16, cT[:, b.par()], ms_ps[1], s_k)
                        if s == 10 and has(1):
                            b = i + 1
                            if has(-1):
                                wait(pe, s_res, (i - 1).count(TT, TT))
                            else:
                                wait(pe, s_xlo, (i + 2).count(1, 1))
                            for t in range(TT):
                                n = 0
                                for k in range(DC):
                                    for pw, px in PASSES:
                                        ins = mm(ms_ps[0][:, t, :], cT[:, b.par(), px, k, t * P:(t + 1) * P],
                                                 wv16[:, pw, k, :], start=(n == 0), stop=(n == 5 and not bias))
                                        n += 1
                                if bias:
                                    for part in range(2):
                                        ins = mm(ms_ps[0][:, t, :], ones16[:, :], bv16[:, part, :],
                                                 start=False, stop=(part == 1))
                            ins.then_inc(s_v, 1)
                        if s == 12 and has(1):
                            b = i + 1
                            wait(pe, s_max, b.count(H, H))
                            if has(2):
                                wait(pe, s_klo, (i + 2).count(1, 1))
                            else:
                                wait(pe, s_on, (i - 1).count(2, 2))
                            for t in range(TT):
                                ins = pe.transpose(ms_ps[1][0:H, 0, t * P:(t + 1) * P], mx[:, b.par(), t, :],
                                                   ident[:, :])
                            ins.then_inc(s_mt, 1)
                        if s == 13 and has(0):
                            if has(1):
                                wait(pe, s_vev, (i + 1).count(1, 1))
                            else:
                                wait(pe, s_res, (i - 1).count(TT, TT))
                            out_transposed(0, 0)
                        if has(0):
                            scores(s)
                        if has(1):
                            for h in max_slots(s):
                                scores_max(h)
                        if s in (6, 10, 14) and has(0):
                            values((s - 6) // 4)
                    if has(0):
                        values(NG - 1)

                bodies(pe, body)

        clear(nc, sems)


TM = 512
TQ = TM // P
NE = 8
FE = 512
FT = 1024


def ternary_mlp(nc, tag, NT, x_in, w_upT, w_downT, gate, x_out):
    NF = FT // P
    x_t = x_in.rearrange("(b t p) d -> b p t d", t=TQ, p=P)
    o_t = x_out.rearrange("(b t p) d -> b p t d", t=TQ, p=P)
    sems = []
    with ExitStack() as ctx:
        def sb(name, shape, dt):
            return ctx.enter_context(nc.sbuf_tensor(f"{tag}_{name}", shape, dt))

        def pb(name, shape, dt):
            return ctx.enter_context(nc.psum_tensor(f"{tag}_{name}", shape, dt))

        def sem(name):
            sems.append(ctx.enter_context(nc.semaphore(f"{tag}_{name}")))
            return sems[-1]

        wu32 = sb("wu32", [P, DC * FT], F32)
        wd32 = sb("wd32", [P, NF * D], F32)
        wabs = sb("wabs", [P, DC * FT], F32)
        wneg = sb("wneg", [P, DC * FT], F16)
        wu16 = sb("wu16", [P, DC, FT], F16)
        wd16 = sb("wd16", [P, NF, D], F16)
        wsum = sb("wsum", [P, 2], F32)
        thr = sb("thr", [P, 4], F32)
        ident = sb("ident", [P, P], F32)
        ones = sb("ones", [P, P], F32)
        expo = sb("expo", [P, 2, TQ], F32)
        tg = sb("tg", [P, 1], F32)
        xin = sb("xin", [P, 2, TQ, D], F32)
        xres = sb("xres", [P, 2, TQ, D], F32)
        bns = sb("bns", [P, TQ, 6], F32)
        mv = sb("mv", [P, TQ, 2], F32)
        vpe = sb("vpe", [P, TQ], F32)
        rstd = sb("rstd", [P, TQ], F32)
        sd = sb("sd", [P, TQ], F32)
        den = sb("den", [P, TQ], F32)
        rden = sb("rden", [P, TQ], F32)
        scl = sb("scl", [P, TQ], F32)
        xn = sb("xn", [P, TQ, D], F32)
        xT = sb("xT", [P, 2, DC, TM], F16)
        h32 = sb("h32", [P, 2, TM], F32)
        hsq = sb("hsq", [P, 2, TM], F32)
        hT = sb("hT", [P, 2, 2, NF, TM], F16)
        ssq = sb("ssq", [P, 2, TM], F32)
        msq = sb("msq", [P, TQ], F32)
        rms = sb("rms", [P, TQ], F32)
        rinv = sb("rinv", [P, TQ], F32)
        oscl = sb("oscl", [P, TQ], F32)

        t_ps = [pb(f"t_ps{i}", [P, TM], F32) for i in range(DC)]
        u_ps = [pb(f"u_ps{i}", [P, TM], F32) for i in range(2)]
        d_ps = [pb(f"d_ps{i}", [P, 2, D], F32) for i in range(2)]
        s_ps = pb("s_ps", [P, TQ], F32)

        alone = sem("alone")
        l_w = sem("l_w")
        c_pool = sem("c_pool")
        c_dve = sem("c_dve")
        c_sum = sem("c_sum")
        c_tanh = sem("c_tanh")
        l_x = [sem(f"l_x{i}") for i in range(2)]
        l_r = [sem(f"l_r{i}") for i in range(2)]
        st_o = [sem(f"st_o{i}") for i in range(2)]
        s_bn = sem("s_bn")
        s_pow = sem("s_pow")
        s_scl = sem("s_scl")
        s_xn = sem("s_xn")
        s_xt = sem("s_xt")
        s_xhi = sem("s_xhi")
        s_xlo = sem("s_xlo")
        s_u = sem("s_u")
        s_h = sem("s_h")
        s_sq = sem("s_sq")
        s_hhi = sem("s_hhi")
        s_hlo = sem("s_hlo")
        s_acc = sem("s_acc")
        s_ms = sem("s_ms")
        s_msq = sem("s_msq")
        s_rms = sem("s_rms")
        s_os = sem("s_os")
        s_d = sem("s_d")
        s_res = sem("s_res")

        LOOP = (3, NT - 3)

        def bodies(eng, body):
            for c in range(-2, LOOP[0]):
                body(At(None, c), lambda n, c=c: 0 <= c + n < NT)
            with eng.Fori(0, (LOOP[1] - LOOP[0]) // 2) as it:
                for u in range(2):
                    body(At(it, LOOP[0] + u), lambda n: True)
            for c in range(LOOP[1], NT + 1):
                body(At(None, c), lambda n, c=c: 0 <= c + n < NT)

        with nc.Block() as block:

            @block.sync
            def _(sp):
                sp.dma_start(wu32[:, :].rearrange("p (k n) -> p k n", k=DC),
                             w_upT.rearrange("(k p) n -> p k n", p=P)).then_inc(l_w, 16)
                sp.dma_start(wd32[:, :].rearrange("p (k n) -> p k n", k=NF),
                             w_downT.rearrange("(k p) n -> p k n", p=P)).then_inc(l_w, 16)
                sp.dma_start(tg[:, :], gate.rearrange("(a n) -> a n", a=1).broadcast_to([P, 1])).then_inc(l_w, 16)

                def body(i, has):
                    if has(2):
                        b = i + 2
                        wait(sp, s_xn, (b - 2).count(TQ, TQ), alone)
                        sp.dma_start(xin[:, b.par()], x_t[b.index()]).then_inc(l_x[b.par()], 16)
                    if has(0):
                        wait(sp, st_o[i.par()], (i - 2).half(16, 16), alone)
                        sp.dma_start(xres[:, i.par()], x_t[i.index()]).then_inc(l_r[i.par()], 16)
                    if has(-1):
                        b = i - 1
                        wait(sp, s_res, b.count(TQ, TQ), alone)
                        sp.dma_start(o_t[b.index()], xres[:, b.par()]).then_inc(st_o[b.par()], 16)

                bodies(sp, body)
                for p in range(2):
                    sp.wait_ge(st_o[p], 16 * (NT // 2))

            @block.gpsimd
            def _(pool):
                pool.memset(ident[:, :], 0.0).then_inc(c_pool, 1)
                pool.memset(ones[:, :], 1.0).then_inc(c_pool, 1)
                pool.memset(expo[:, 0, :], -0.5).then_inc(c_pool, 1)
                pool.memset(expo[:, 1, :], 0.5).then_inc(c_pool, 1)
                pool.wait_ge(c_pool, 4)
                pool.affine_select(out=ident[:, :], in_=ident[:, :], compare_op=ALU.not_equal, fill=1.0,
                                   base=0, pattern=[[-1, P]], channel_multiplier=1).then_inc(c_pool, 1)

                def body(i, has):
                    if has(-1):
                        b = i - 1
                        wait(pool, s_msq, b.count(1, 1), alone)
                        wait(pool, s_os, (b - 1).count(3, 1), alone)
                        pool.tensor_tensor(rms[:, :], msq[:, :], expo[:, 1, :], ALU.pow).then_inc(s_rms, 1)
                    if has(0):
                        for f in range(NF):
                            wait(pool, s_sq, i.count(NF, f + 1), alone)
                            if f == 0:
                                wait(pool, s_ms, (i - 2).count(1, 1), alone)
                                pool.tensor_scalar(ssq[:, i.par()], hsq[:, f % 2], 1.0, None,
                                                   ALU.mult).then_inc(s_acc, 1)
                            else:
                                wait(pool, s_acc, i.count(NF, f), alone)
                                pool.tensor_tensor(ssq[:, i.par()], ssq[:, i.par()], hsq[:, f % 2],
                                                   ALU.add).then_inc(s_acc, 1)
                            if f == 5 and has(2):
                                variances(i + 2)
                    elif has(2):
                        variances(i + 2)

                def variances(b):
                    wait(pool, s_bn, b.count(2 * TQ, 2 * TQ), alone)
                    wait(pool, s_scl, (b - 1).count(4, 4), alone)
                    pool.tensor_scalar(vpe[:, :], mv[:, :, 1], EPS, None, ALU.add).then_inc(s_pow, 1)
                    pool.tensor_tensor(sd[:, :], mv[:, :, 1], expo[:, 1, :], ALU.pow).then_inc(s_pow, 1)
                    wait(pool, s_pow, b.count(3, 2), alone)
                    pool.tensor_tensor(rstd[:, :], vpe[:, :], expo[:, 0, :], ALU.pow).then_inc(s_pow, 1)

                bodies(pool, body)

            @block.scalar
            def _(act):
                act.wait_ge(l_w, 48)
                act.activation(tg[:, :], tg[:, :], ACT.Tanh).then_inc(c_tanh, 1)

                def body(i, has):
                    def x_hi():
                        b = i + 1
                        wait(act, s_u, i.count(NF, NF))
                        for k in range(DC):
                            wait(act, s_xt, b.count(DC, k + 1))
                            act.activation(xT[:, HI, k], t_ps[k][:, :], ACT.Identity).then_inc(s_xhi, 1)

                    if has(0):
                        for f in range(NF):
                            n = i.count(NF, f)
                            wait(act, s_u, i.count(NF, f + 1))
                            wait(act, s_sq, i.count(NF, f - 1))
                            wait(act, s_hlo, i.count(NF, f - 1))
                            act.activation(h32[:, f % 2], u_ps[f % 2][:, :], ACT.Gelu).then_inc(s_h, 1)
                            wait(act, s_h, i.count(NF, f + 1))
                            wait(act, s_acc, i.count(NF, f - 1))
                            act.activation(hsq[:, f % 2], h32[:, f % 2], ACT.Square).then_inc(s_sq, 1)
                    if has(1):
                        x_hi()

                bodies(act, body)

            @block.vector
            def _(dve):
                n = 0
                dve.wait_ge(l_w, 48)
                for j, w in enumerate((wu32, wd32)):
                    dve.scalar_tensor_tensor(wabs[:, :], w[:, :], -1.0, w[:, :], ALU.mult,
                                             ALU.max).then_inc(c_dve, 1)
                    dve.wait_ge(c_dve, n + 1)
                    dve.tensor_reduce(wsum[:, j:j + 1], wabs[:, :], AX_X, ALU.add).then_inc(c_dve, 1)
                    dve.wait_ge(c_dve, n + 2)
                    n += 2
                dve.wait_ge(c_sum, 1)
                dve.tensor_scalar(thr[:, 0:2], s_ps[:, 0:2], 0.5 / (D * FT), None, ALU.mult).then_inc(c_dve, 1)
                dve.tensor_scalar(thr[:, 2:4], s_ps[:, 0:2], -0.5 / (D * FT), None, ALU.mult).then_inc(c_dve, 1)
                dve.wait_ge(c_dve, n + 2)
                n += 2
                for j, (w, w16) in enumerate(((wu32, wu16), (wd32, wd16))):
                    flat = w16[:, :, :].rearrange("p k n -> p (k n)")
                    dve.tensor_scalar(wneg[:, :], w[:, :], thr[:, 2 + j:3 + j], None, ALU.is_lt).then_inc(c_dve, 1)
                    dve.wait_ge(c_dve, n + 1)
                    dve.scalar_tensor_tensor(flat, w[:, :], thr[:, j:j + 1], wneg[:, :], ALU.is_gt,
                                             ALU.subtract).then_inc(c_dve, 1)
                    dve.wait_ge(c_dve, n + 2)
                    n += 2
                dve.wait_ge(c_tanh, 1)

                def statistics(b):
                    wait(dve, l_x[b.par()], b.half(16, 16))
                    wait(dve, s_xn, (b - 1).count(TQ, TQ))
                    for t in range(TQ):
                        dve.bn_stats(bns[:, t, :], xin[:, b.par(), t]).then_inc(s_bn, 1)
                    for t in range(TQ):
                        wait(dve, s_bn, b.count(2 * TQ, t + 1), alone)
                        dve.bn_aggr(mv[:, t, :], bns[:, t, :]).then_inc(s_bn, 1)

                def normalise(b):
                    wait(dve, s_pow, b.count(3, 3))
                    dve.tensor_tensor(den[:, :], sd[:, :], rstd[:, :], ALU.mult).then_inc(s_scl, 1)
                    wait(dve, s_scl, b.count(4, 1))
                    dve.tensor_scalar(den[:, :], den[:, :], 1e-8, None, ALU.add).then_inc(s_scl, 1)
                    wait(dve, s_scl, b.count(4, 2))
                    dve.reciprocal(rden[:, :], den[:, :]).then_inc(s_scl, 1)
                    wait(dve, s_scl, b.count(4, 3))
                    dve.tensor_tensor(scl[:, :], rden[:, :], rstd[:, :], ALU.mult).then_inc(s_scl, 1)
                    wait(dve, s_scl, b.count(4, 4))
                    wait(dve, s_xt, (b - 1).count(DC, DC))
                    for t in range(TQ):
                        dve.tensor_scalar(xn[:, t], xin[:, b.par(), t], mv[:, t, 0:1], scl[:, t:t + 1],
                                          ALU.subtract, ALU.mult).then_inc(s_xn, 1)

                def body(i, has):
                    for f in range(NF):
                        if has(0):
                            n = i.count(NF, f + 1)
                            wait(dve, s_h, n)
                            if f == 0:
                                wait(dve, s_d, (i - 2).count(2, 2))
                            dve.tensor_copy(hT[:, i.par(), HI, f], h32[:, f % 2]).then_inc(s_hhi, 1)
                            wait(dve, s_hhi, n)
                            dve.tensor_tensor(hT[:, i.par(), LO, f], h32[:, f % 2], hT[:, i.par(), HI, f],
                                              ALU.subtract).then_inc(s_hlo, 1)
                        if f == 0 and has(-1):
                            b = i - 1
                            wait(dve, s_ms, b.count(1, 1))
                            dve.tensor_scalar(msq[:, :], s_ps[:, :], 1.0 / FT, None, ALU.mult).then_inc(s_msq, 1)
                        if f == 2 and has(-1):
                            b = i - 1
                            wait(dve, s_rms, b.count(1, 1))
                            dve.tensor_scalar(oscl[:, :], rms[:, :], 1e-8, None, ALU.add).then_inc(s_os, 1)
                            wait(dve, s_os, b.count(3, 1))
                            dve.reciprocal(rinv[:, :], oscl[:, :]).then_inc(s_os, 1)
                            wait(dve, s_os, b.count(3, 2))
                            dve.tensor_scalar(oscl[:, :], rinv[:, :], tg[:, 0:1], None, ALU.mult).then_inc(s_os, 1)
                            wait(dve, s_os, b.count(3, 3))
                        if f in (4, NF - 1) and has(-1):
                            b = i - 1
                            k = 0 if f == 4 else 1
                            wait(dve, s_d, b.count(2, k + 1))
                            wait(dve, l_r[b.par()], b.half(16, 16))
                            for t in (2 * k, 2 * k + 1):
                                dve.scalar_tensor_tensor(xres[:, b.par(), t], d_ps[k][:, t % 2, :],
                                                         oscl[:, t:t + 1], xres[:, b.par(), t],
                                                         ALU.mult, ALU.add).then_inc(s_res, 1)
                        if f == 3 and has(2):
                            statistics(i + 2)
                        if f == 6 and has(2):
                            normalise(i + 2)
                    if has(1):
                        b = i + 1
                        for k in range(DC):
                            wait(dve, s_xhi, b.count(DC, k + 1))
                            dve.tensor_tensor(xT[:, LO, k], t_ps[k][:, :], xT[:, HI, k],
                                              ALU.subtract).then_inc(s_xlo, 1)

                bodies(dve, body)

            @block.tensor
            def _(pe):
                mm = nc.tensor.matmul
                pe.wait_ge(c_dve, 4)
                pe.wait_ge(c_pool, 5)
                mm(s_ps[:, 0:2], ones[:, :], wsum[:, :], start=True, stop=True).then_inc(c_sum, 1)
                pe.wait_ge(c_dve, 10)

                def down(b, t):
                    n = 0
                    for f in range(NF):
                        for part in range(2):
                            ins = mm(d_ps[t // 2][:, t % 2, :], hT[:, b.par(), part, f, t * P:(t + 1) * P],
                                     wd16[:, f, :], start=(n == 0), stop=(n == 2 * NF - 1))
                            n += 1
                    if t % 2:
                        ins.then_inc(s_d, 1)

                def body(i, has):
                    if has(-1):
                        b = i - 1
                        wait(pe, s_acc, b.count(NF, NF))
                        wait(pe, s_msq, (b - 1).count(1, 1))
                        for t in range(TQ):
                            ins = mm(s_ps[:, t:t + 1], ssq[:, b.par(), t * P:(t + 1) * P], ones[:, 0:1],
                                     start=True, stop=True)
                        ins.then_inc(s_ms, 1)
                    for f in range(NF):
                        if has(0):
                            if f == 0:
                                wait(pe, s_xlo, i.count(DC, DC))
                            wait(pe, s_h, i.count(NF, f - 1))
                            n = 0
                            for k in range(DC):
                                for part in range(2):
                                    ins = mm(u_ps[f % 2][:, :], wu16[:, k, f * P:(f + 1) * P], xT[:, part, k, :],
                                             start=(n == 0), stop=(n == 3))
                                    n += 1
                            ins.then_inc(s_u, 1)
                        if f % 2 and has(-1):
                            b = i - 1
                            t = f // 2
                            if t == 0:
                                wait(pe, s_hlo, b.count(NF, NF))
                            if t % 2 == 0:
                                wait(pe, s_res, (b - 1).count(TQ, t + 2))
                            down(b, t)
                        if f == 6 and has(1):
                            b = i + 1
                            wait(pe, s_xn, b.count(TQ, TQ))
                            wait(pe, s_xlo, (b - 1).count(DC, DC))
                            for k in range(DC):
                                for t in range(TQ):
                                    ins = pe.transpose(t_ps[k][:, t * P:(t + 1) * P],
                                                       xn[:, t, k * P:(k + 1) * P], ident[:, :])
                                ins.then_inc(s_xt, 1)

                bodies(pe, body)

        clear(nc, sems)


def moe(nc, tag, NT, x_in, wg, wu, wd, w1, w2, gate, out):
    T = NT * TM
    NC = T // P
    NTE = 2 * T // TM + NE - 1
    NS = NTE * TM
    NF = FE // P
    PAD = 1 << 20
    WN = DC * FE
    x_t = x_in.rearrange("(b t p) d -> b p t d", t=TQ, p=P)
    o_t = out.rearrange("(b t p) d -> b p t d", t=TQ, p=P)
    wu_e = wu.rearrange("e (k p) n -> e p k n", p=P)
    wd_e = wd.rearrange("e (k p) n -> e p k n", p=P)
    xn_d = nc.dram_tensor(f"{tag}_xn_dram", (T, D), F32, kind="Internal").ap()
    xn_t = xn_d.rearrange("(b t p) d -> b p t d", t=TQ, p=P)
    wu_s = nc.dram_tensor(f"{tag}_wu_dram", (NE, P, 2, WN), F16, kind="Internal").ap()
    wd_s = nc.dram_tensor(f"{tag}_wd_dram", (NE, P, 2, WN), F16, kind="Internal").ap()
    table = nc.dram_tensor(f"{tag}_table", (NS, 2), I32, kind="Internal").ap()
    table_t = table.rearrange("(b t p) w -> b p t w", t=TQ, p=P)

    sems = []
    with ExitStack() as ctx:
        def sb(name, shape, dt, c=ctx):
            return c.enter_context(nc.sbuf_tensor(f"{tag}_{name}", shape, dt))

        def pb(name, shape, dt, c=ctx):
            return c.enter_context(nc.psum_tensor(f"{tag}_{name}", shape, dt))

        def sem(name):
            sems.append(ctx.enter_context(nc.semaphore(f"{tag}_{name}")))
            return sems[-1]

        def loop_bodies(eng, body, first, lo, hi, n):
            for c in range(first, lo):
                body(At(None, c), lambda k, c=c: 0 <= c + k < n)
            with eng.Fori(0, (hi - lo) // 2) as it:
                for u in range(2):
                    body(At(it, lo + u), lambda k: True)
            for c in range(hi, n + 1):
                body(At(None, c), lambda k, c=c: 0 <= c + k < n)

        ident = sb("ident", [P, P], F32)
        tg = sb("tg", [P, 1], F32)
        te = sb("te", [1, NTE + 1], I32)
        alone = sem("alone")
        c_pool = sem("c_pool")

        early = ctx.enter_context(ExitStack())
        xall = sb("xall", [P, 2, DC, T], F16, early)
        lg = sb("lg", [P, NC, NE], F32, early)
        pair = sb("pair", [P, NC, 2, 2], I32, early)
        slot = sb("slot", [P, NC, 2], I32, early)

        with ExitStack() as c1:
            wgl = sb("wgl", [P, DC, NE], F32, c1)
            wg16 = sb("wg16", [P, 2, DC, NE], F16, c1)
            half_neg = sb("half_neg", [P, TQ], F32, c1)
            pads = sb("pads", [P, NS // P, 2], I32, c1)
            xin = sb("xin", [P, 2, TQ, D], F32, c1)
            bns = sb("bns", [P, TQ, 6], F32, c1)
            mv = sb("mv", [P, TQ, 2], F32, c1)
            vpe = sb("vpe", [P, TQ], F32, c1)
            rstd = sb("rstd", [P, TQ], F32, c1)
            xn = sb("xn", [P, 2, TQ, D], F32, c1)
            w32 = sb("w32", [P, 2, WN], F32, c1)
            w16 = sb("w16", [P, 2, 2, WN], F16, c1)
            t_ps = [[pb(f"rt_ps{i}{k}", [P, TM], F32, c1) for k in range(DC)] for i in range(2)]
            l_ps = [pb(f"l_ps{i}", [P, TQ, NE], F32, c1) for i in range(2)]
            l_w = sem("l_w")
            c_tanh = sem("c_tanh")
            c_dve = sem("c_dve")
            l_x = [sem(f"rl_x{i}") for i in range(2)]
            l_e = [sem(f"rl_e{i}") for i in range(2)]
            st_n = [sem(f"st_n{i}") for i in range(2)]
            st_w = [sem(f"st_w{i}") for i in range(2)]
            st_t = sem("st_t")
            s_bn = sem("r_bn")
            s_rstd = sem("r_rstd")
            s_xn = sem("r_xn")
            s_xt = sem("r_xt")
            s_xhi = sem("r_xhi")
            s_xlo = sem("r_xlo")
            s_l = sem("r_l")
            s_lg = sem("r_lg")
            s_whi = sem("r_whi")
            s_wlo = sem("r_wlo")
            assert NT == 2 * NE

            def bodies(eng, body):
                loop_bodies(eng, body, -2, 2, NT - 2, NT)

            def job(b):
                src, dst = ((wu_e, wu_s), (wd_e, wd_s))[b.par()]
                e = b.c // 2 if b.it is None else b.it + b.c // 2
                return src[e], dst[e]

            with nc.Block() as block:
                @block.sync
                def _(sp):
                    sp.dma_start(wgl[:, :, :], wg.rearrange("(k p) n -> p k n", p=P)).then_inc(l_w, 16)
                    sp.dma_start(tg[:, :], gate.rearrange("(a n) -> a n", a=1).broadcast_to([P, 1])).then_inc(l_w, 16)
                    sp.wait_ge(c_pool, 5)
                    sp.dma_start(table.rearrange("(p n) w -> p n w", p=P), pads[:, :, :]).then_inc(st_t, 16)

                    def body(i, has):
                        if has(2):
                            b = i + 2
                            wait(sp, s_xn, (b - 2).count(TQ, TQ), alone)
                            sp.dma_start(xin[:, b.par()], x_t[b.index()]).then_inc(l_x[b.par()], 16)
                        if has(1):
                            b = i + 1
                            src = job(b)[0]
                            wait(sp, s_wlo, (b - 2).count(1, 1), alone)
                            sp.dma_start(w32[:, b.par()].rearrange("p (k n) -> p k n", k=src.shape[1]),
                                         src).then_inc(l_e[b.par()], 16)
                            wait(sp, s_xn, b.count(TQ, TQ), alone)
                            sp.dma_start(xn_t[b.index()], xn[:, b.par()]).then_inc(st_n[b.par()], 16)
                        if has(0):
                            wait(sp, s_wlo, i.count(1, 1), alone)
                            sp.dma_start(job(i)[1], w16[:, i.par()]).then_inc(st_w[i.par()], 16)

                    bodies(sp, body)
                    sp.wait_ge(st_t, 16)
                    for p in range(2):
                        sp.wait_ge(st_n[p], 16 * (NT // 2))
                        sp.wait_ge(st_w[p], 16 * (NT // 2))

                @block.gpsimd
                def _(pool):
                    pool.memset(ident[:, :], 0.0).then_inc(c_pool, 1)
                    pool.memset(half_neg[:, :], -0.5).then_inc(c_pool, 1)
                    pool.memset(pads[:, :, :], PAD).then_inc(c_pool, 1)
                    pool.wait_ge(c_pool, 3)
                    pool.affine_select(out=ident[:, :], in_=ident[:, :], compare_op=ALU.not_equal, fill=1.0,
                                       base=0, pattern=[[-1, P]], channel_multiplier=1).then_inc(c_pool, 1)
                    pool.memset(pads[:, :, 1], 0).then_inc(c_pool, 1)

                    def body(i, has):
                        if has(1):
                            b = i + 1
                            wait(pool, s_bn, b.count(2 * TQ, 2 * TQ), alone)
                            wait(pool, s_xn, (b - 1).count(TQ, TQ), alone)
                            pool.tensor_scalar(vpe[:, :], mv[:, :, 1], EPS, None, ALU.add).then_inc(s_rstd, 1)
                            wait(pool, s_rstd, b.count(2, 1), alone)
                            pool.tensor_tensor(rstd[:, :], vpe[:, :], half_neg[:, :], ALU.pow).then_inc(s_rstd, 1)

                    bodies(pool, body)
                    for c in range(2):
                        pool.iota(pair[:, :, c, 0], pattern=[[P, NC]], base=0, channel_multiplier=1)\
                            .then_inc(c_pool, 1)

                @block.scalar
                def _(act):
                    act.wait_ge(l_w, 32)
                    act.activation(tg[:, :], tg[:, :], ACT.Tanh).then_inc(c_tanh, 1)

                    def body(i, has):
                        if has(0):
                            for k in range(DC):
                                wait(act, s_xt, i.count(DC, k + 1))
                                act.activation(xall[:, HI, k, bass.ds(i.index() * TM, TM)],
                                               t_ps[i.par()][k][:, :], ACT.Identity).then_inc(s_xhi, 1)
                            wait(act, l_e[i.par()], i.half(16, 16))
                            wait(act, st_w[i.par()], (i - 2).half(16, 16))
                            act.activation(w16[:, i.par(), HI], w32[:, i.par()], ACT.Identity,
                                           scale=WS).then_inc(s_whi, 1)

                    bodies(act, body)

                @block.vector
                def _(dve):
                    dve.wait_ge(l_w, 32)
                    split_weight(dve, c_dve, 0, wgl[:, :, :], wg16, WS)
                    dve.wait_ge(c_dve, 3)

                    def body(i, has):
                        if has(1):
                            b = i + 1
                            wait(dve, l_x[b.par()], b.half(16, 16))
                            for t in range(TQ):
                                dve.bn_stats(bns[:, t, :], xin[:, b.par(), t]).then_inc(s_bn, 1)
                            for t in range(TQ):
                                wait(dve, s_bn, b.count(2 * TQ, t + 1), alone)
                                dve.bn_aggr(mv[:, t, :], bns[:, t, :]).then_inc(s_bn, 1)
                        if has(0):
                            for k in range(DC):
                                wait(dve, s_xhi, i.count(DC, k + 1))
                                cols = bass.ds(i.index() * TM, TM)
                                dve.tensor_tensor(xall[:, LO, k, cols], t_ps[i.par()][k][:, :],
                                                  xall[:, HI, k, cols], ALU.subtract).then_inc(s_xlo, 1)
                            wait(dve, s_whi, i.count(1, 1))
                            dve.scalar_tensor_tensor(w16[:, i.par(), LO], w32[:, i.par()], WS,
                                                     w16[:, i.par(), HI], ALU.mult,
                                                     ALU.subtract).then_inc(s_wlo, 1)
                        if has(1):
                            b = i + 1
                            wait(dve, s_rstd, b.count(2, 2))
                            wait(dve, s_xt, (b - 2).count(DC, DC))
                            wait(dve, st_n[b.par()], (b - 2).half(16, 16))
                            for t in range(TQ):
                                dve.tensor_scalar(xn[:, b.par(), t], xin[:, b.par(), t], mv[:, t, 0:1],
                                                  rstd[:, t:t + 1], ALU.subtract, ALU.mult).then_inc(s_xn, 1)
                        if has(0):
                            wait(dve, s_l, i.count(1, 1))
                            dve.tensor_scalar(lg[:, bass.ds(i.index() * TQ, TQ), :], l_ps[i.par()][:, :, :],
                                              1.0 / WS, None, ALU.mult).then_inc(s_lg, 1)

                    bodies(dve, body)

                @block.tensor
                def _(pe):
                    mm = nc.tensor.matmul
                    pe.wait_ge(c_pool, 4)
                    pe.wait_ge(c_dve, 3)

                    def body(i, has):
                        if has(1):
                            b = i + 1
                            wait(pe, s_xn, b.count(TQ, TQ))
                            wait(pe, s_xlo, (b - 2).count(DC, DC))
                            for k in range(DC):
                                for t in range(TQ):
                                    ins = pe.transpose(t_ps[b.par()][k][:, t * P:(t + 1) * P],
                                                       xn[:, b.par(), t, k * P:(k + 1) * P], ident[:, :])
                                ins.then_inc(s_xt, 1)
                        if has(0):
                            wait(pe, s_xlo, i.count(DC, DC))
                            wait(pe, s_lg, (i - 2).count(1, 1))
                            for t in range(TQ):
                                n = 0
                                for k in range(DC):
                                    for pw, px in PASSES:
                                        ins = mm(l_ps[i.par()][:, t, :],
                                                 xall[:, px, k, bass.ds(i.index() * TM + t * P, P)],
                                                 wg16[:, pw, k, :], start=(n == 0), stop=(n == 5))
                                        n += 1
                            ins.then_inc(s_l, 1)

                    bodies(pe, body)

        with ExitStack() as c2:
            def arr(name):
                return sb(name, [P, NC, NE], F32, c2)

            ie = arr("ie")
            eq = arr("eq")
            oh = [arr("oh1"), arr("oh2")]
            l2 = arr("l2")
            hot16 = sb("hot16", [P, NC, NE], F16, c2)
            below = sb("below", [P, P], F16, c2)
            ones16 = sb("ones16", [P, P], F16, c2)
            cum = [arr("cum0"), arr("cum1")]
            tot = arr("tot")
            pos = arr("pos")
            tmp = arr("tmp")
            m = [sb(f"m{i}", [P, NC], F32, c2) for i in range(2)]
            sc = [sb(f"sc{i}", [P, NC], F32, c2) for i in range(2)]
            ex = sb("ex", [P, NC], F32, c2)
            dn = sb("dn", [P, NC], F32, c2)
            w = [sb(f"w{i}", [P, NC], F32, c2) for i in range(2)]
            cnt = sb("cnt", [P, NE], F32, c2)
            cnti = sb("cnti", [P, NE], I32, c2)
            tiles = [sb(f"tiles{i}", [P, NE], F32, c2) for i in range(2)]
            ntile = sb("ntile", [P, NE], F32, c2)
            tid = sb("tid", [1, NTE + 1, NE], F32, c2)
            tcmp = sb("tcmp", [1, NTE + 1, NE], F32, c2)
            tef = sb("tef", [1, NTE + 1], F32, c2)
            z_ps = [pb(f"z_ps{i}", [P, NC * NE], F32, c2) for i in range(2)]
            q_pool = sem("q_pool")
            q_pe = sem("q_pe")
            q_act = sem("q_act")
            q_dve = sem("q_dve")
            at = {}

            with nc.Block() as block:
                @block.gpsimd
                def _(pool):
                    pool.iota(ie[:, :, :], pattern=[[0, NC], [-1, NE]], base=NE, channel_multiplier=0,
                              allow_small_or_imprecise_dtypes=True).then_inc(q_pool, 1)
                    pool.iota(tid[:, :, :], pattern=[[1, NTE + 1], [0, NE]], base=0, channel_multiplier=0,
                              allow_small_or_imprecise_dtypes=True).then_inc(q_pool, 1)
                    pool.memset(ones16[:, :], 1.0).then_inc(q_pool, 1)
                    pool.memset(below[:, :], 1.0).then_inc(q_pool, 1)
                    pool.wait_ge(q_pool, 4)
                    pool.affine_select(out=below[:, :], in_=below[:, :], compare_op=ALU.is_gt, fill=0.0,
                                       base=0, pattern=[[1, P]], channel_multiplier=-1).then_inc(q_pool, 1)

                @block.vector
                def _(dve):
                    n = [0]

                    def step(ins, name=None):
                        n[0] += 1
                        if name:
                            at[name] = n[0]
                        ins.then_inc(q_dve, 1)
                        dve.wait_ge(q_dve, n[0])

                    def over_e(v):
                        return v[:, :].unsqueeze(2).broadcast_to([P, NC, NE])

                    dve.wait_ge(q_pool, 5)
                    src = lg
                    for c in range(2):
                        step(dve.tensor_reduce(m[c][:, :], src[:, :, :], AX_X, ALU.max))
                        step(dve.tensor_tensor(eq[:, :, :], src[:, :, :], over_e(m[c]), ALU.is_equal))
                        step(dve.tensor_tensor(eq[:, :, :], eq[:, :, :], ie[:, :, :], ALU.mult))
                        step(dve.tensor_reduce(sc[c][:, :], eq[:, :, :], AX_X, ALU.max))
                        step(dve.tensor_tensor(oh[c][:, :, :], ie[:, :, :], over_e(sc[c]), ALU.is_equal))
                        if c == 0:
                            step(dve.scalar_tensor_tensor(
                                l2[:, :, :].rearrange("p t e -> p (t e)"),
                                oh[0][:, :, :].rearrange("p t e -> p (t e)"), -3e38,
                                lg[:, :, :].rearrange("p t e -> p (t e)"), ALU.mult, ALU.add))
                            src = l2
                    step(dve.tensor_tensor(m[1][:, :], m[1][:, :], m[0][:, :], ALU.subtract), "diff")
                    step(dve.tensor_tensor(hot16[:, :, :], oh[0][:, :, :], oh[1][:, :, :], ALU.add), "hot")
                    dve.wait_ge(q_act, 1)
                    step(dve.tensor_scalar(dn[:, :], ex[:, :], 1.0, None, ALU.add))
                    step(dve.reciprocal(w[0][:, :], dn[:, :]))
                    step(dve.tensor_tensor(w[1][:, :], w[0][:, :], ex[:, :], ALU.mult))
                    for c in range(2):
                        step(dve.tensor_scalar(pair[:, :, c, 1].bitcast(F32), w[c][:, :], tg[:, 0:1], 1.0 / WS,
                                               ALU.mult, ALU.mult))
                    dve.wait_ge(q_pe, 1)
                    step(dve.tensor_copy(tot[:, :, :].rearrange("p t e -> p (t e)"), z_ps[0][:, :]))
                    a, b = tot, cum[0]
                    s = 1
                    while s < NC:
                        step(dve.tensor_tensor(b[:, s:, :], a[:, s:, :], a[:, :NC - s, :], ALU.add))
                        step(dve.tensor_copy(b[:, :s, :], a[:, :s, :]))
                        a, b = b, (cum[1] if b is cum[0] else cum[0])
                        s *= 2
                    step(dve.tensor_scalar(cnt[:, :], a[:, NC - 1, :], float(TM - 1), None, ALU.add))
                    step(dve.tensor_copy(cnti[:, :], cnt[:, :]))
                    step(dve.tensor_scalar(cnti[:, :], cnti[:, :], TM.bit_length() - 1, None,
                                           ALU.arith_shift_right))
                    step(dve.tensor_copy(ntile[:, :], cnti[:, :]))
                    ta, tb = ntile, tiles[0]
                    s = 1
                    while s < NE:
                        step(dve.tensor_tensor(tb[:, s:], ta[:, s:], ta[:, :NE - s], ALU.add))
                        step(dve.tensor_copy(tb[:, :s], ta[:, :s]))
                        ta, tb = tb, (tiles[1] if tb is tiles[0] else tiles[0])
                        s *= 2
                    step(dve.tensor_tensor(tcmp[:, :, :], tid[:, :, :],
                                           ta[0:1, :].unsqueeze(1).broadcast_to([1, NTE + 1, NE]), ALU.is_ge))
                    step(dve.tensor_reduce(tef[:, :], tcmp[:, :, :], AX_X, ALU.add))
                    step(dve.tensor_scalar(tef[:, :], tef[:, :], float(NE - 1), None, ALU.min))
                    step(dve.tensor_copy(te[:, :], tef[:, :]))
                    step(dve.tensor_tensor(cnt[:, :], ta[:, :], ntile[:, :], ALU.subtract))
                    step(dve.tensor_scalar(cnt[:, :], cnt[:, :], float(TM), None, ALU.mult))
                    step(dve.tensor_tensor(pos[:, :, :], a[:, :, :], tot[:, :, :], ALU.subtract))
                    step(dve.tensor_tensor(pos[:, :, :], pos[:, :, :],
                                           cnt[:, :].unsqueeze(1).broadcast_to([P, NC, NE]), ALU.add))
                    step(dve.tensor_tensor(pos[:, :, :].rearrange("p t e -> p (t e)"),
                                           pos[:, :, :].rearrange("p t e -> p (t e)"), z_ps[1][:, :], ALU.add))
                    for c in range(2):
                        step(dve.tensor_tensor(tmp[:, :, :], pos[:, :, :], oh[c][:, :, :], ALU.mult))
                        step(dve.tensor_reduce(sc[c][:, :], tmp[:, :, :], AX_X, ALU.add))
                        step(dve.tensor_copy(slot[:, :, c], sc[c][:, :]))

                @block.scalar
                def _(act):
                    act.wait_ge(q_dve, 12)
                    act.activation(ex[:, :], m[1][:, :], ACT.Exp).then_inc(q_act, 1)

                @block.tensor
                def _(pe):
                    pe.wait_ge(q_pool, 5)
                    pe.wait_ge(q_dve, 13)
                    flat = hot16[:, :, :].rearrange("p t e -> p (t e)")
                    nc.tensor.matmul(z_ps[0][:, :], ones16[:, :], flat, start=True, stop=True)
                    nc.tensor.matmul(z_ps[1][:, :], below[:, :], flat, start=True, stop=True).then_inc(q_pe, 1)

            assert at == {"diff": 12, "hot": 13}

        with ExitStack() as c3:
            s32 = sb("s32", [P, WN], F32, c3)
            s1 = sb("s1", [P, 2, DC, FE], F16, c3)
            s2 = sb("s2", [P, 2, NF, D], F16, c3)
            tgs = sb("tgs", [P, 1], F32, c3)
            xres = sb("xres", [P, 2, TQ, D], F32, c3)
            h32 = sb("h32", [P, 2, TM], F32, c3)
            hT = sb("hT", [P, 2, 2, NF, TM], F16, c3)
            idx = sb("idx", [P, 2, 2], I32, c3)
            ent = sb("ent", [P, 2, 2, 2], I32, c3)
            u_ps = [pb(f"su_ps{i}", [P, TM], F32, c3) for i in range(2)]
            d_ps = [pb(f"sd_ps{i}", [P, 2, D], F32, c3) for i in range(2)]
            l_w = [sem(f"h_lw{i}") for i in range(2)]
            c_dve = sem("h_dve")
            l_r = [sem(f"h_lr{i}") for i in range(2)]
            st_o = [sem(f"h_st{i}") for i in range(2)]
            s_u = sem("h_u")
            s_h = sem("h_h")
            s_hhi = sem("h_hhi")
            s_hlo = sem("h_hlo")
            s_d = sem("h_d")
            s_res = sem("h_res")
            g_copy = sem("g_copy")
            g_put = [sem(f"g_put{i}") for i in range(2)]

            def bodies(eng, body):
                loop_bodies(eng, body, 0, 2, NT, NT)

            with nc.Block() as block:
                @block.sync
                def _(sp):
                    sp.dma_start(s32[:, :].rearrange("p (k n) -> p k n", k=DC),
                                 w1.rearrange("(k p) n -> p k n", p=P)).then_inc(l_w[0], 16)
                    sp.wait_ge(c_dve, 3)
                    sp.dma_start(s32[:, :].rearrange("p (k n) -> p k n", k=NF),
                                 w2.rearrange("(k p) n -> p k n", p=P)).then_inc(l_w[1], 16)

                    def body(i, has):
                        if has(0):
                            wait(sp, st_o[i.par()], (i - 2).half(16, 16), alone)
                            sp.dma_start(xres[:, i.par()], x_t[i.index()]).then_inc(l_r[i.par()], 16)
                        if has(-1):
                            b = i - 1
                            wait(sp, s_res, b.count(TQ, TQ), alone)
                            sp.dma_start(o_t[b.index()], xres[:, b.par()]).then_inc(st_o[b.par()], 16)

                    bodies(sp, body)
                    for p in range(2):
                        sp.wait_ge(st_o[p], 16 * (NT // 2))

                @block.gpsimd
                def _(pool):
                    def put(b, first):
                        p = b.par()
                        if not first:
                            wait(pool, g_put[p], (b - 2).half(32, 32), alone)
                        pool.tensor_copy(idx[:, p, :], slot[:, b.index(), :]).then_inc(g_copy, 1)
                        pool.tensor_copy(ent[:, p], pair[:, b.index()]).then_inc(g_copy, 1)
                        wait(pool, g_copy, b.count(2, 2), alone)
                        for c in range(2):
                            pool.indirect_dma_start(table, bass.IndirectOffsetOnAxis(idx[:, p, c:c + 1], 0),
                                                    ent[:, p, c, :], None).then_inc(g_put[p], 16)

                    put(At(None, 0), True)
                    put(At(None, 1), True)
                    with pool.Fori(0, NC // 2 - 1) as it:
                        for u in range(2):
                            put(At(it, 2 + u), False)
                    for p in range(2):
                        pool.wait_ge(g_put[p], 32 * (NC // 2))

                @block.scalar
                def _(act):
                    def body(i, has):
                        if has(0):
                            for f in range(NF):
                                wait(act, s_u, i.count(NF, f + 1))
                                wait(act, s_hlo, i.count(NF, f - 1))
                                act.activation(h32[:, f % 2], u_ps[f % 2][:, :], ACT.Gelu,
                                               scale=1.0 / WS).then_inc(s_h, 1)

                    bodies(act, body)

                @block.vector
                def _(dve):
                    dve.wait_ge(l_w[0], 16)
                    n = split_weight(dve, c_dve, 0, s32[:, :], s1.ap().rearrange("p a k n -> p a (k n)"), WS)
                    dve.wait_ge(l_w[1], 16)
                    n = split_weight(dve, c_dve, n, s32[:, :], s2.ap().rearrange("p a k n -> p a (k n)"), WS)
                    dve.tensor_scalar(tgs[:, :], tg[:, :], 1.0 / WS, None, ALU.mult).then_inc(c_dve, 1)
                    dve.wait_ge(c_dve, n + 1)

                    def body(i, has):
                        for f in range(NF):
                            if has(0):
                                n = i.count(NF, f + 1)
                                wait(dve, s_h, n)
                                if f == 0:
                                    wait(dve, s_d, (i - 2).count(2, 2))
                                dve.tensor_copy(hT[:, i.par(), HI, f], h32[:, f % 2]).then_inc(s_hhi, 1)
                                wait(dve, s_hhi, n)
                                dve.tensor_tensor(hT[:, i.par(), LO, f], h32[:, f % 2], hT[:, i.par(), HI, f],
                                                  ALU.subtract).then_inc(s_hlo, 1)
                            if f in (2, NF - 1) and has(-1):
                                b = i - 1
                                k = 0 if f == 2 else 1
                                wait(dve, s_d, b.count(2, k + 1))
                                wait(dve, l_r[b.par()], b.half(16, 16))
                                for t in (2 * k, 2 * k + 1):
                                    dve.scalar_tensor_tensor(xres[:, b.par(), t], d_ps[k][:, t % 2, :],
                                                             tgs[:, 0:1], xres[:, b.par(), t],
                                                             ALU.mult, ALU.add).then_inc(s_res, 1)

                    bodies(dve, body)

                @block.tensor
                def _(pe):
                    mm = nc.tensor.matmul
                    pe.wait_ge(c_dve, 7)

                    def body(i, has):
                        for f in range(NF):
                            if has(0):
                                wait(pe, s_h, i.count(NF, f - 1))
                                n = 0
                                for k in range(DC):
                                    for pw, px in PASSES:
                                        ins = mm(u_ps[f % 2][:, :], s1[:, pw, k, f * P:(f + 1) * P],
                                                 xall[:, px, k, bass.ds(i.index() * TM, TM)],
                                                 start=(n == 0), stop=(n == 5))
                                        n += 1
                                ins.then_inc(s_u, 1)
                            if has(-1):
                                b = i - 1
                                if f == 0:
                                    wait(pe, s_hlo, b.count(NF, NF))
                                if f % 2 == 0:
                                    wait(pe, s_res, (b - 1).count(TQ, f + 2))
                                n = 0
                                for g in range(NF):
                                    for pw, px in PASSES:
                                        ins = mm(d_ps[f // 2][:, f % 2, :],
                                                 hT[:, b.par(), px, g, f * P:(f + 1) * P], s2[:, pw, g, :],
                                                 start=(n == 0), stop=(n == 3 * NF - 1))
                                        n += 1
                                if f % 2:
                                    ins.then_inc(s_d, 1)

                    bodies(pe, body)
        early.close()

        with ExitStack() as c4:
            tab = sb("tab", [P, 2, TQ, 2], I32, c4)
            tab2 = sb("tab2", [P, 2, TQ, 2], I32, c4)
            gix = sb("gix", [P, 2, TQ], I32, c4)
            xg = sb("xg", [P, 2, TQ, D], F32, c4)
            xT = sb("exT", [P, 2, DC, TM], F16, c4)
            up = sb("up", [P, 2, 2, DC, FE], F16, c4)
            dn = sb("dnw", [P, 2, 2, NF, D], F16, c4)
            h32 = sb("eh32", [P, 2, TM], F32, c4)
            hT = sb("ehT", [P, 2, 2, NF, TM], F16, c4)
            y = sb("y", [P, 2, TQ, D], F32, c4)
            t_ps = [pb(f"et_ps{k}", [P, TM], F32, c4) for k in range(DC)]
            u_ps = [pb(f"eu_ps{i}", [P, TM], F32, c4) for i in range(2)]
            d_ps = [pb(f"ed_ps{i}", [P, 2, D], F32, c4) for i in range(2)]
            l_t = [sem(f"e_lt{i}") for i in range(2)]
            l_t2 = [sem(f"e_ltt{i}") for i in range(2)]
            l_u = [sem(f"e_lu{i}") for i in range(2)]
            l_d = [sem(f"e_ld{i}") for i in range(2)]
            g_x = [sem(f"e_gx{i}") for i in range(2)]
            g_y = [sem(f"e_gy{i}") for i in range(2)]
            s_ix = sem("e_ix")
            s_xt = sem("e_xt")
            s_xhi = sem("e_xhi")
            s_xlo = sem("e_xlo")
            s_u = sem("e_u")
            s_h = sem("e_h")
            s_hhi = sem("e_hhi")
            s_hlo = sem("e_hlo")
            s_d = sem("e_d")
            s_y = sem("e_y")

            def bodies(eng, body):
                loop_bodies(eng, body, -2, 3, NTE - 2, NTE)

            assert NTE % 2

            with nc.Block() as block:
                @block.sync
                def _(sp):
                    def body(i, has):
                        if has(2):
                            b = i + 2
                            wait(sp, s_ix, (b - 2).count(1, 1), alone)
                            sp.dma_start(tab[:, b.par()], table_t[b.index()]).then_inc(l_t[b.par()], 16)
                        if has(0):
                            wait(sp, g_y[i.par()], (i - 2).half(16 * TQ, 16 * TQ), alone)
                            sp.dma_start(tab2[:, i.par()], table_t[i.index()]).then_inc(l_t2[i.par()], 16)
                        if has(1):
                            b = i + 1
                            e = sp.value_load(te[0:1, bass.ds(b.index(), 1)], min_val=0, max_val=NE - 1)
                            wait(sp, s_u, (b - 2).count(NF, NF), alone)
                            sp.dma_start(up[:, b.par()].rearrange("p a k n -> p a (k n)"),
                                         wu_s[e]).then_inc(l_u[b.par()], 16)
                            wait(sp, s_d, (b - 2).count(2, 2), alone)
                            sp.dma_start(dn[:, b.par()].rearrange("p a k n -> p a (k n)"),
                                         wd_s[e]).then_inc(l_d[b.par()], 16)

                    bodies(sp, body)

                @block.gpsimd
                def _(pool):
                    def body(i, has):
                        if has(2):
                            b = i + 2
                            p = b.par()
                            wait(pool, s_ix, b.count(1, 1), alone)
                            wait(pool, s_xt, (b - 2).count(DC, DC), alone)
                            for t in range(TQ):
                                pool.indirect_dma_start(xg[:, p, t], None, xn_d,
                                                        bass.IndirectOffsetOnAxis(gix[:, p, t:t + 1], 0))\
                                    .then_inc(g_x[p], 16)
                        if has(-1):
                            b = i - 1
                            p = b.par()
                            wait(pool, s_y, b.count(TQ, TQ), alone)
                            wait(pool, g_y[1 - p], (b - 1).half(16 * TQ, 16 * TQ), alone)
                            for t in range(TQ):
                                pool.indirect_dma_start(out, bass.IndirectOffsetOnAxis(tab2[:, p, t, 0:1], 0),
                                                        y[:, p, t], None, bounds_check=T - 1, oob_is_err=False,
                                                        compute_op=ALU.add).then_inc(g_y[p], 16)

                    bodies(pool, body)
                    pool.wait_ge(g_y[0], 16 * TQ * ((NTE + 1) // 2))
                    pool.wait_ge(g_y[1], 16 * TQ * (NTE // 2))

                @block.scalar
                def _(act):
                    def body(i, has):
                        if has(0):
                            for f in range(NF):
                                wait(act, s_u, i.count(NF, f + 1))
                                wait(act, s_hlo, i.count(NF, f - 1))
                                act.activation(h32[:, f % 2], u_ps[f % 2][:, :], ACT.Gelu,
                                               scale=1.0 / WS).then_inc(s_h, 1)
                        if has(1):
                            b = i + 1
                            wait(act, s_u, i.count(NF, NF))
                            for k in range(DC):
                                wait(act, s_xt, b.count(DC, k + 1))
                                act.activation(xT[:, HI, k], t_ps[k][:, :], ACT.Identity).then_inc(s_xhi, 1)

                    bodies(act, body)

                @block.vector
                def _(dve):
                    def body(i, has):
                        def results(k):
                            b = i - 1
                            p = b.par()
                            wait(dve, s_d, b.count(2, k + 1))
                            if k == 0:
                                wait(dve, l_t2[p], b.half(16, 16))
                                wait(dve, g_y[p], (b - 2).half(16 * TQ, 16 * TQ))
                            for t in (2 * k, 2 * k + 1):
                                dve.tensor_scalar(y[:, p, t], d_ps[k][:, t % 2, :],
                                                  tab2[:, p, t, 1:2].bitcast(F32), None,
                                                  ALU.mult).then_inc(s_y, 1)

                        if has(2):
                            b = i + 2
                            p = b.par()
                            wait(dve, l_t[p], b.half(16, 16))
                            wait(dve, g_x[p], (b - 2).half(16 * TQ, 16 * TQ))
                            dve.tensor_scalar(gix[:, p], tab[:, p, :, 0], T - 1, None,
                                              ALU.min).then_inc(s_ix, 1)
                        for f in range(NF):
                            if has(0):
                                n = i.count(NF, f + 1)
                                wait(dve, s_h, n)
                                if f == 0:
                                    wait(dve, s_d, (i - 2).count(2, 2))
                                dve.tensor_copy(hT[:, i.par(), HI, f], h32[:, f % 2]).then_inc(s_hhi, 1)
                                wait(dve, s_hhi, n)
                                dve.tensor_tensor(hT[:, i.par(), LO, f], h32[:, f % 2], hT[:, i.par(), HI, f],
                                                  ALU.subtract).then_inc(s_hlo, 1)
                            if f in (2, NF - 1) and has(-1):
                                results(0 if f == 2 else 1)
                        if has(1):
                            b = i + 1
                            for k in range(DC):
                                wait(dve, s_xhi, b.count(DC, k + 1))
                                dve.tensor_tensor(xT[:, LO, k], t_ps[k][:, :], xT[:, HI, k],
                                                  ALU.subtract).then_inc(s_xlo, 1)

                    bodies(dve, body)

                @block.tensor
                def _(pe):
                    mm = nc.tensor.matmul

                    def body(i, has):
                        for f in range(NF):
                            if has(0):
                                if f == 0:
                                    wait(pe, l_u[i.par()], i.half(16, 16))
                                    wait(pe, s_xlo, i.count(DC, DC))
                                wait(pe, s_h, i.count(NF, f - 1))
                                n = 0
                                for k in range(DC):
                                    for pw, px in PASSES:
                                        ins = mm(u_ps[f % 2][:, :], up[:, i.par(), pw, k, f * P:(f + 1) * P],
                                                 xT[:, px, k, :], start=(n == 0), stop=(n == 5))
                                        n += 1
                                ins.then_inc(s_u, 1)
                            if has(-1):
                                b = i - 1
                                if f == 0:
                                    wait(pe, l_d[b.par()], b.half(16, 16))
                                    wait(pe, s_hlo, b.count(NF, NF))
                                if f % 2 == 0:
                                    wait(pe, s_y, (b - 1).count(TQ, f + 2))
                                n = 0
                                for g in range(NF):
                                    for pw, px in PASSES:
                                        ins = mm(d_ps[f // 2][:, f % 2, :],
                                                 hT[:, b.par(), px, g, f * P:(f + 1) * P],
                                                 dn[:, b.par(), pw, g, :], start=(n == 0), stop=(n == 3 * NF - 1))
                                        n += 1
                                if f % 2:
                                    ins.then_inc(s_d, 1)
                            if f == 2 and has(1):
                                b = i + 1
                                wait(pe, g_x[b.par()], b.half(16 * TQ, 16 * TQ))
                                wait(pe, s_xlo, (b - 1).count(DC, DC))
                                for k in range(DC):
                                    for t in range(TQ):
                                        ins = pe.transpose(t_ps[k][:, t * P:(t + 1) * P],
                                                           xg[:, b.par(), t, k * P:(k + 1) * P], ident[:, :])
                                    ins.then_inc(s_xt, 1)

                    bodies(pe, body)

        clear(nc, sems)


def gated_transformer(nc, a, out):
    T = a["x"].shape[0]
    NB = T // S
    x1 = nc.dram_tensor("x1", (T, D), F32, kind="Internal").ap()
    x2 = nc.dram_tensor("x2", (T, D), F32, kind="Internal").ap()
    x3 = nc.dram_tensor("x3", (T, D), F32, kind="Internal").ap()
    attention(nc, "a0", NB, a["x"], a["ctxT"], a["L0_WqT"], a["L0_WkT"], a["L0_WvT"], a["L0_WoT"], None,
              a["g_xattn"][0:1], x1)
    ternary_mlp(nc, "f0", T // TM, x1, a["L0_w_upT"], a["L0_w_downT"], a["g_ffn"][0:1], x2)
    attention(nc, "a1", NB, x2, a["ctxT"], a["L1_Wq"], a["L1_Wk"], a["L1_Wv"], a["L1_Wo"],
              (a["L1_bqT"], a["L1_bkT"], a["L1_bv"], a["L1_bo"]), a["g_xattn"][1:2], x3)
    moe(nc, "m1", T // TM, x3, a["L1_Wg"], a["L1_Wu"], a["L1_Wd"], a["L1_W1"], a["L1_W2"], a["g_ffn"][1:2], out)


def kernel(**inputs):
    import numpy as _np
    import concourse.bacc as _bacc
    from concourse import mybir as _mybir
    from concourse.bass_utils import run_bass_kernel_spmd as _run

    v = {n: _np.asarray(x) for n, x in inputs.items()}
    shape = v["x"].shape
    tokens = shape[0] * shape[1]
    laid = {
        "x": v["x"].reshape(tokens, D),
        "ctxT": v["ctx_1024"].reshape(tokens, D).T,
        "g_xattn": v["g_xattn"],
        "g_ffn": v["g_ffn"],
        "L0_WqT": v["L0_xattn_Wq"].T,
        "L0_WkT": v["L0_xattn_Wk"].T,
        "L0_WvT": v["L0_xattn_Wv"].T,
        "L0_WoT": v["L0_xattn_Wo"].T,
        "L0_w_upT": v["L0_ffn_w_up"].T,
        "L0_w_downT": v["L0_ffn_w_down"].T,
        "L1_Wq": v["L1_xattn_Wq"],
        "L1_Wk": v["L1_xattn_Wk"],
        "L1_Wv": v["L1_xattn_Wv"],
        "L1_Wo": v["L1_xattn_Wo"],
        "L1_bqT": v["L1_xattn_bq"].reshape(DC, P).T,
        "L1_bkT": v["L1_xattn_bk"].reshape(DC, P).T,
        "L1_bv": v["L1_xattn_bv"],
        "L1_bo": v["L1_xattn_bo"],
        "L1_Wg": v["L1_ffn_Wg"],
        "L1_Wu": v["L1_ffn_Wu"],
        "L1_Wd": v["L1_ffn_Wd"],
        "L1_W1": v["L1_ffn_W1"],
        "L1_W2": v["L1_ffn_W2"],
    }
    nc = _bacc.Bacc("TRN2", target_bir_lowering=False, num_devices=1)
    arrays, args = {}, {}
    for name, value in laid.items():
        value = _np.ascontiguousarray(value)
        arrays[f"in_{name}"] = value
        args[name] = nc.dram_tensor(f"in_{name}", value.shape, _mybir.dt.from_np(value.dtype),
                                    kind="ExternalInput").ap()
    out = nc.dram_tensor("out_0", (tokens, D), F32, kind="ExternalOutput").ap()
    gated_transformer(nc, args, out)
    r = _run(nc, [arrays], core_ids=[0])
    return _np.asarray(r.results[0]["out_0"]).reshape(shape)
```

```python
from contextlib import ExitStack

import numpy as np

import concourse.bass as bass
from concourse import mybir

F32 = mybir.dt.float32
F16 = mybir.dt.float16
I32 = mybir.dt.int32
U32 = mybir.dt.uint32
ACT = mybir.ActivationFunctionType
ALU = mybir.AluOpType
AX_X = mybir.AxisListType.X

P = 128
D = 256
DC = D // P
S = 256
TT = S // P
H = 16
DH = D // H
G = 4
NG = H // G
HI, LO = 0, 1
WS = 16.0
MS = 64.0
EPS = 1e-5
PASSES = ((HI, HI), (LO, HI), (HI, LO))


def clear(nc, sems):
    with nc.Block() as block:
        @block.gpsimd
        def _(pool):
            for s in sems:
                pool.sem_clear(s)


class At:

    def __init__(self, it, c):
        self.it, self.c = it, c

    def __add__(self, n):
        return At(self.it, self.c + n)

    def __sub__(self, n):
        return At(self.it, self.c - n)

    def par(self):
        return self.c % 2

    def index(self):
        return self.c if self.it is None else self.it * 2 + self.c

    def count(self, per, k):
        v = per * self.c + k
        return v if self.it is None else self.it * (2 * per) + v

    def half(self, per, k):
        v = per * (self.c // 2) + k
        return v if self.it is None else self.it * per + v


def is_body(i, c):
    return i.it is None and i.c == c


def wait(eng, sem, value, alone=None):
    if isinstance(value, int) and value <= 0:
        return
    eng.wait_ge(sem, value)
    if alone is not None and not isinstance(value, int):
        eng.sem_inc(alone, 1)


def split_weight(dve, sem, n, w32, w16, scale):
    dve.tensor_scalar(w32, w32, scale, None, ALU.mult).then_inc(sem, 1)
    dve.wait_ge(sem, n + 1)
    dve.tensor_copy(w16[:, HI], w32).then_inc(sem, 1)
    dve.wait_ge(sem, n + 2)
    dve.tensor_tensor(w16[:, LO], w32, w16[:, HI], ALU.subtract).then_inc(sem, 1)
    return n + 3


def attention(nc, tag, NB, x_in, ctxT, wqT, wkT, wvT, woT, bias, gate, x_out):
    x_b = x_in.rearrange("(b t p) d -> b p t d", t=TT, p=P)
    o_b = x_out.rearrange("(b t p) d -> b p t d", t=TT, p=P)
    c_b = ctxT.rearrange("(k p) (b s) -> b p k s", p=P, s=S)
    pack_q = nc.dram_tensor(f"{tag}_pack_q", (2, 2, DH, H, S), F16, kind="Internal").ap()
    pack_k = nc.dram_tensor(f"{tag}_pack_k", (2, 2, DH, H, S), F16, kind="Internal").ap()
    HH = H // 2

    sems = []
    with ExitStack() as ctx:
        def sb(name, shape, dt):
            return ctx.enter_context(nc.sbuf_tensor(f"{tag}_{name}", shape, dt))

        def pb(name, shape, dt):
            return ctx.enter_context(nc.psum_tensor(f"{tag}_{name}", shape, dt))

        def sem(name):
            sems.append(ctx.enter_context(nc.semaphore(f"{tag}_{name}")))
            return sems[-1]

        wq16 = sb("wq16", [P, 2, DC, D], F16)
        wk16 = sb("wk16", [P, 2, DC, D], F16)
        wv16 = sb("wv16", [P, 2, DC, D], F16)
        wo16 = sb("wo16", [P, 2, DC, D], F16)
        wq32 = sb("wq32", [P, DC, D], F32)
        wk32 = sb("wk32", [P, DC, D], F32)
        wv32 = sb("wv32", [P, DC, D], F32)
        wo32 = sb("wo32", [P, DC, D], F32)
        ident = sb("ident", [P, P], F32)
        half_neg = sb("half_neg", [P, TT], F32)
        tg = sb("tg", [P, 1], F32)
        if bias:
            bqk = sb("bqk", [P, 2, DC], F32)
            bv32 = sb("bv32", [1, D], F32)
            bv16 = sb("bv16", [1, 2, D], F16)
            ones16 = sb("ones16", [1, P], F16)
            bo = sb("bo", [P, D], F32)
        xin = sb("xin", [P, 2, TT, D], F32)
        cin = sb("cin", [P, 2, DC, S], F32)
        xres = sb("xres", [P, 2, TT, D], F32)
        bns = sb("bns", [P, TT, 6], F32)
        mv = sb("mv", [P, TT, 2], F32)
        vpe = sb("vpe", [P, TT], F32)
        rstd = sb("rstd", [P, TT], F32)
        xn = sb("xn", [P, TT, D], F32)
        xT = sb("xT", [P, 2, DC, S], F16)
        cT = sb("cT", [P, 2, 2, DC, S], F16)
        qT = sb("qT", [P, 2, DC, S], F16)
        kT = sb("kT", [P, 2, DC, S], F16)
        Qp = sb("Qp", [P, 2, H, S], F16)
        Kp = sb("Kp", [P, 2, H, S], F16)
        Qm = sb("Qm", [P, 2, H, S], F16)
        V = sb("V", [P, 2, TT, H, 32], F32)
        mx = sb("mx", [P, 2, TT, H], F32)
        mrow = sb("mrow", [H, 2, S], F16)
        pr = sb("pr", [P, 2 * G, TT, S], F32)
        ou = sb("ou", [P, NG, S], F32)
        rinv = sb("rinv", [P, 2, 2 * H // 2], F32)
        on = sb("on", [P, TT, D], F32)
        oT = sb("oT", [P, 2, DC, S], F16)

        mx_ps = [pb(f"mx_ps{i}", [P, TT, S], F32) for i in range(3)]
        st_ps = [pb(f"st_ps{i}", [P, TT, S], F32) for i in range(2)]
        pv_ps = pb("pv_ps", [P, 2 * S], F32)
        ms_ps = [pb(f"ms_ps{i}", [P, TT, S], F32) for i in range(2)]

        alone = sem("alone")
        l_w = sem("l_w")
        l_wo = sem("l_wo")
        c_pool = sem("c_pool")
        c_rows = sem("c_rows")
        c_act = sem("c_act")
        c_tanh = sem("c_tanh")
        c_dve = sem("c_dve")
        l_x = [sem(f"l_x{i}") for i in range(2)]
        l_c = [sem(f"l_c{i}") for i in range(2)]
        l_r = [sem(f"l_r{i}") for i in range(2)]
        st_o = [sem(f"st_o{i}") for i in range(2)]
        d_pack = [sem(f"d_pack{i}") for i in range(2)]
        d_a = [sem(f"d_a{i}") for i in range(2)]
        d_b = [sem(f"d_b{i}") for i in range(2)]
        d_m = [sem(f"d_m{i}") for i in range(2)]
        s_bn = sem("s_bn")
        s_rstd = sem("s_rstd")
        s_xn = sem("s_xn")
        s_xt = sem("s_xt")
        s_xhi = sem("s_xhi")
        s_xlo = sem("s_xlo")
        s_ct = sem("s_ct")
        s_q = sem("s_q")
        s_qhi = sem("s_qhi")
        s_qlo = sem("s_qlo")
        s_k = sem("s_k")
        s_khi = sem("s_khi")
        s_klo = sem("s_klo")
        s_v = sem("s_v")
        s_vev = sem("s_vev")
        s_mm = sem("s_mm")
        s_max = sem("s_max")
        s_mt = sem("s_mt")
        s_mrow = sem("s_mrow")
        s_st = sem("s_st")
        s_exp = sem("s_exp")
        s_pv = sem("s_pv")
        s_ou = sem("s_ou")
        s_at = sem("s_at")
        s_rinv = sem("s_rinv")
        s_on = sem("s_on")
        s_bt = sem("s_bt")
        s_ohi = sem("s_ohi")
        s_olo = sem("s_olo")
        s_o = sem("s_o")
        s_bo = sem("s_bo")
        s_res = sem("s_res")

        weights = ((wq32, wq16), (wk32, wk16), (wv32, wv16), (wo32, wo16))
        n_dve = len(weights) + (6 if bias else 1)
        n_early = 4 if bias else 3

        BODIES = range(-3, NB + 1)
        LOOP = (3, NB - 3)

        def bodies(eng, body):
            for c in range(BODIES[0], LOOP[0]):
                body(At(None, c), lambda n, c=c: 0 <= c + n < NB)
            with eng.Fori(0, (LOOP[1] - LOOP[0]) // 2) as it:
                for u in range(2):
                    body(At(it, LOOP[0] + u), lambda n: True)
            for c in range(LOOP[1], NB + 1):
                body(At(None, c), lambda n, c=c: 0 <= c + n < NB)

        AT = dict(p=5, r=6, l=14, n=15, x=0, q=4, a1=5, k=7, b=8, o=12, y=12, a0=15, m=13, v=15, M=13)

        def grouped(s, first):
            n, g = divmod(s - first, G * NG)
            return (n, g // G) if g % G == 0 else (n, None)

        def max_slots(s):
            return [h for h in range(H) if h * AT['M'] // H == s]

        with nc.Block() as block:

            @block.sync
            def _(sp):
                def load_x(b):
                    wait(sp, s_xn, (b - 2).count(TT, TT), alone)
                    sp.dma_start(xin[:, b.par()], x_b[b.index()]).then_inc(l_x[b.par()], 16)

                def load_c(b):
                    wait(sp, s_ct, (b - 2).count(2, 2), alone)
                    sp.dma_start(cin[:, b.par()], c_b[b.index()]).then_inc(l_c[b.par()], 16)

                def pack(b, half):
                    p, h0 = b.par(), half * HH
                    hs = slice(h0, h0 + HH)
                    done = (d_a, d_b)[half][p]
                    for r in range(2):
                        sp.dma_start(Qp[32 * r:32 * r + 32, p, hs, :],
                                     pack_q[p, :, :, hs, :].rearrange("a d h s -> (a d) h s")).then_inc(done, 16)
                        sp.dma_start(Kp[32 * r:32 * r + 32, p, hs, :],
                                     pack_k[p, r:r + 1, :, hs, :].broadcast_to([2, DH, HH, S])).then_inc(done, 16)
                    sp.dma_start(Qm[0:DH, p, hs, :], pack_q[p, HI, :, hs, :]).then_inc(done, 16)

                def body(i, has):
                    if has(3):
                        load_x(i + 3)
                        load_c(i + 3)
                    if is_body(i, -3):
                        for w32, w in ((wq32, wqT), (wk32, wkT), (wv32, wvT), (wo32, woT)):
                            sp.dma_start(w32[:, :, :], w.rearrange("(k p) n -> p k n", p=P)).then_inc(l_w, 16)
                        if bias:
                            for n in range(2):
                                sp.dma_start(bqk[:, n, :], bias[n]).then_inc(l_wo, 16)
                            sp.dma_start(bv32[:, :], bias[2].rearrange("(a n) -> a n", a=1)).then_inc(l_wo, 16)
                            sp.dma_start(bo[:, :], bias[3].rearrange("(a n) -> a n", a=1).broadcast_to([P, D])).then_inc(l_wo, 16)
                        sp.dma_start(tg[:, :], gate.rearrange("(a n) -> a n", a=1).broadcast_to([P, 1])).then_inc(l_wo, 16)
                    if has(0):
                        b = i
                        wait(sp, st_o[b.par()], (b - 2).half(16, 16), alone)
                        sp.dma_start(xres[:, b.par()], x_b[b.index()]).then_inc(l_r[b.par()], 16)
                    if has(2):
                        b = i + 2
                        wait(sp, d_a[b.par()], (b - 2).half(80, 80), alone)
                        wait(sp, d_b[b.par()], (b - 2).half(80, 80), alone)
                        for t16, hi, lo, dram in ((qT, s_qhi, s_qlo, pack_q), (kT, s_khi, s_klo, pack_k)):
                            wait(sp, hi, b.count(1, 1), alone)
                            wait(sp, lo, b.count(1, 1), alone)
                            for part in range(2):
                                sp.dma_start(
                                    dram[b.par(), part].rearrange("d (t h) s -> h d t s", t=DC),
                                    t16[:, part]).then_inc(d_pack[b.par()], 16)
                    if has(2):
                        b = i + 2
                        wait(sp, d_pack[b.par()], b.half(64, 64), alone)
                        wait(sp, s_mm, i.count(H, H), alone)
                        wait(sp, s_st, i.count(H, HH), alone)
                        if not has(0):
                            sp.wait_ge(c_rows, 1)
                        pack(b, 0)
                    if has(-1):
                        b = i - 1
                        wait(sp, s_res, b.count(TT, TT), alone)
                        sp.dma_start(o_b[b.index()], xres[:, b.par()]).then_inc(st_o[b.par()], 16)
                    if has(2):
                        wait(sp, s_st, i.count(H, H), alone)
                        pack(i + 2, 1)

                bodies(sp, body)
                for p in range(2):
                    sp.wait_ge(st_o[p], 16 * (NB // 2))

            @block.gpsimd
            def _(pool):
                pool.memset(ident[:, :], 0.0).then_inc(c_pool, 1)
                pool.wait_ge(c_pool, 1)
                pool.affine_select(out=ident[:, :], in_=ident[:, :], compare_op=ALU.not_equal, fill=1.0,
                                   base=0, pattern=[[-1, P]], channel_multiplier=1).then_inc(c_pool, 1)
                pool.memset(half_neg[:, :], -0.5).then_inc(c_pool, 1)
                if bias:
                    pool.memset(ones16[:, :], 1.0).then_inc(c_pool, 1)
                pool.wait_ge(c_pool, n_early)

                def body(i, has):
                    if has(2):
                        b = i + 2
                        p = b.par()
                        wait(pool, l_c[p], b.half(16, 16), alone)
                        wait(pool, s_v, (b - 2).count(1, 1), alone)
                        pool.tensor_copy(cT[:, p, HI], cin[:, p]).then_inc(s_ct, 1)
                        wait(pool, s_ct, b.count(2, 1), alone)
                        pool.tensor_tensor(cT[:, p, LO], cin[:, p], cT[:, p, HI], ALU.subtract).then_inc(s_ct, 1)

                    if has(-1) and bias:
                        b = i - 1
                        wait(pool, l_r[b.par()], b.half(16, 16), alone)
                        for t in range(TT):
                            pool.tensor_tensor(xres[:, b.par(), t], xres[:, b.par(), t], bo[:, :],
                                               ALU.add).then_inc(s_bo, 1)
                    if is_body(i, -2):
                        pool.wait_ge(s_ct, 2)
                        pool.memset(Kp[64:P, :, :, :], MS).then_inc(c_pool, 1)
                        pool.wait_ge(c_pool, n_early + 1)
                        pool.memset(V[:, :, :, :, :], WS).then_inc(c_pool, 1)
                        pool.wait_ge(c_pool, n_early + 2)
                    if has(3):
                        b = i + 3
                        wait(pool, s_bn, b.count(2 * TT, 2 * TT), alone)
                        wait(pool, s_xn, (b - 1).count(TT, TT), alone)
                        pool.tensor_scalar(vpe[:, :], mv[:, :, 1], EPS, None, ALU.add).then_inc(s_rstd, 1)
                        wait(pool, s_rstd, b.count(2, 1), alone)
                        pool.tensor_tensor(rstd[:, :], vpe[:, :], half_neg[:, :], ALU.pow).then_inc(s_rstd, 1)

                bodies(pool, body)

            @block.scalar
            def _(act):
                def body(i, has):
                    if is_body(i, -2):
                        act.wait_ge(l_w, 64)
                        for w32, w16 in weights:
                            act.activation(w16[:, HI], w32[:, :, :], ACT.Identity, scale=WS).then_inc(c_act, 1)
                        act.wait_ge(l_wo, 16 * (1 + (4 if bias else 0)))
                        act.activation(tg[:, :], tg[:, :], ACT.Tanh).then_inc(c_tanh, 1)
                        act.wait_ge(c_dve, n_dve)
                    if is_body(i, -1):
                        act.wait_ge(c_pool, n_early + 2)
                        act.wait_ge(c_rows, 2)
                    def exp_head(s):
                        b = i
                        wait(act, s_st, b.count(H, s + 1))
                        g = s // G
                        if s % G == 0:
                            wait(act, s_pv, b.count(NG, g - 1))
                        act.activation(pr[:, s % (2 * G)], st_ps[s % 2][:, :, :], ACT.Exp,
                                       scale=DH ** -0.5 / (WS * WS)).then_inc(s_exp, 1)

                    def out_raw(n, g):
                        b = i + n
                        wait(act, s_pv, b.count(NG, g + 1))
                        if g % 2 == 0:
                            wait(act, s_at, (b - 1).count(2, g // 2 + 1))
                        act.activation(ou[:, g, :], pv_ps[:, 0:S], ACT.Identity).then_inc(s_ou, 1)

                    def qk_hi(src, dst, there, done, n):
                        b = i + 2
                        wait(act, there, b.count(1, 1))
                        wait(act, d_pack[(b - 1).par()], (b - 1).half(64, 64))
                        if bias:
                            for t in range(DC):
                                ins = act.activation(dst[:, HI, t, :], src[:, t, :], ACT.Identity,
                                                     bias=bqk[:, n, t:t + 1])
                        else:
                            ins = act.activation(dst[:, HI], src[:, :, :], ACT.Identity)
                        ins.then_inc(done, 1)

                    for s in range(H):
                        if s == AT['x'] and has(2):
                            b = i + 2
                            wait(act, s_xt, b.count(1, 1))
                            wait(act, s_q, (b - 1).count(1, 1))
                            act.activation(xT[:, HI], ms_ps[0][:, :, :], ACT.Identity).then_inc(s_xhi, 1)
                        if s == AT['b'] and has(-1):
                            b = i - 1
                            wait(act, s_bt, b.count(1, 1))
                            wait(act, s_o, (b - 1).count(1, 1))
                            act.activation(oT[:, HI], ms_ps[0][:, :, :], ACT.Identity).then_inc(s_ohi, 1)
                        if s == AT['q'] and has(2):
                            qk_hi(ms_ps[1], qT, s_q, s_qhi, 0)
                        if s == AT['k'] and has(2):
                            qk_hi(ms_ps[1], kT, s_k, s_khi, 1)
                        if has(0):
                            exp_head(s)
                        n, g = grouped(s, AT['r'])
                        if g is not None and has(n):
                            out_raw(n, g)
                        if s == AT['m'] and has(1):
                            b = i + 1
                            wait(act, s_mt, b.count(1, 1))
                            wait(act, d_m[b.par()], (b - 2).half(16, 16))
                            act.activation(mrow[:, b.par(), :], ms_ps[1][0:H, 0, :], ACT.Identity,
                                           scale=-1.0 / MS).then_inc(s_mrow, 1)
                            wait(act, s_mrow, b.count(1, 1))
                            act.dma_start(Qp[64:65, b.par()], mrow[:, b.par(), :]).then_inc(d_m[b.par()], 16)
                        if s == AT['v'] and has(1):
                            b = i + 1
                            wait(act, s_v, b.count(1, 1))
                            wait(act, s_pv, (i - 1).count(NG, NG))
                            act.activation(V[:, b.par(), :, :, 0:DH],
                                           ms_ps[1][:, :, :].rearrange("p t (h d) -> p t h d", d=DH),
                                           ACT.Identity).then_inc(s_vev, 1)

                bodies(act, body)

            @block.vector
            def _(dve):
                dve.memset(Qm[:, :, :, :], 0.0).then_inc(c_rows, 1)

                def constants():
                    for n, (w32, w16) in enumerate(weights):
                        dve.wait_ge(c_act, n + 1)
                        dve.scalar_tensor_tensor(w16[:, LO], w32[:, :, :], WS, w16[:, HI], ALU.mult,
                                                 ALU.subtract).then_inc(c_dve, 1)
                    n = len(weights)
                    dve.wait_ge(l_wo, 16 * (1 + (4 if bias else 0)))
                    dve.wait_ge(c_tanh, 1)
                    if bias:
                        dve.tensor_scalar(bo[:, :], bo[:, :], tg[:, 0:1], None, ALU.mult).then_inc(c_dve, 1)
                        dve.tensor_scalar(bqk[:, :, :], bqk[:, :, :], WS, None, ALU.mult).then_inc(c_dve, 1)
                        n = split_weight(dve, c_dve, n + 2, bv32[:, :], bv16, WS)
                    dve.wait_ge(c_dve, n)
                    dve.tensor_scalar(tg[:, :], tg[:, :], 1.0 / WS, None, ALU.mult).then_inc(c_dve, 1)
                    dve.wait_ge(c_dve, n + 1)


                def body(i, has):
                    if is_body(i, -2):
                        constants()
                    if is_body(i, -1):
                        dve.memset(Qp[64:P, :, :, :], 0.0).then_inc(c_rows, 1)
                    def maxima(h):
                        b = i + 1
                        if h == 0:
                            wait(dve, s_mt, (b - 2).count(1, 1))
                        wait(dve, s_mm, b.count(H, h + 1))
                        dve.tensor_reduce(mx[:, b.par(), :, h], mx_ps[h % 3][:, :, :], AX_X,
                                          ALU.max).then_inc(s_max, 1)

                    def normalise(n, k):
                        b = i + n
                        a = ms_ps[0][:, :, :].rearrange("p t (j e) -> p t j e", e=32)
                        wait(dve, s_at, b.count(2, k + 1))
                        dve.reciprocal(rinv[:, k, :].rearrange("p (t j) -> p t j", t=TT),
                                       a[:, :, :, DH]).then_inc(s_rinv, 1)
                        wait(dve, s_rinv, b.count(2, k + 1))
                        if k == 0:
                            wait(dve, s_bt, (b - 1).count(1, 1))
                        for t in range(TT):
                            ins = dve.tensor_tensor(
                                on[:, t, k * P:(k + 1) * P].rearrange("p (j d) -> p j d", d=DH),
                                a[:, t, :, 0:DH],
                                rinv[:, k, t * HH:(t + 1) * HH].unsqueeze(2).broadcast_to([P, HH, DH]),
                                ALU.mult)
                        ins.then_inc(s_on, 1)

                    def qk_lo(src, dst, hi, done, n):
                        b = i + 2
                        wait(dve, hi, b.count(1, 1))
                        if bias:
                            for t in range(DC):
                                ins = dve.scalar_tensor_tensor(dst[:, LO, t, :], src[:, t, :],
                                                               bqk[:, n, t:t + 1], dst[:, HI, t, :],
                                                               ALU.add, ALU.subtract)
                        else:
                            ins = dve.tensor_tensor(dst[:, LO], src[:, :, :], dst[:, HI], ALU.subtract)
                        ins.then_inc(done, 1)

                    for s in range(H):
                        if has(1):
                            for h in max_slots(s):
                                maxima(h)
                        if s == AT['x'] and has(2):
                            wait(dve, s_xhi, (i + 2).count(1, 1))
                            dve.tensor_tensor(xT[:, LO], ms_ps[0][:, :, :], xT[:, HI],
                                              ALU.subtract).then_inc(s_xlo, 1)
                        if s == AT['a1'] and has(-1):
                            normalise(-1, 1)
                        if s == AT['b'] and has(-1):
                            wait(dve, s_ohi, (i - 1).count(1, 1))
                            dve.tensor_tensor(oT[:, LO], ms_ps[0][:, :, :], oT[:, HI],
                                              ALU.subtract).then_inc(s_olo, 1)
                        if s == AT['q'] and has(2):
                            qk_lo(ms_ps[1], qT, s_qhi, s_qlo, 0)
                        if s == AT['y'] and has(-1):
                            b = i - 1
                            wait(dve, s_o, b.count(1, 1))
                            if bias:
                                wait(dve, s_bo, b.count(TT, TT))
                            wait(dve, l_r[b.par()], b.half(16, 16))
                            for t in range(TT):
                                dve.scalar_tensor_tensor(xres[:, b.par(), t], ms_ps[0][:, t, :], tg[:, 0:1],
                                                         xres[:, b.par(), t], ALU.mult, ALU.add).then_inc(s_res, 1)
                        if s == AT['k'] and has(2):
                            qk_lo(ms_ps[1], kT, s_khi, s_klo, 1)
                        if s == AT['a0'] and has(0):
                            normalise(0, 0)
                        if s == AT['l'] and has(3):
                            b = i + 3
                            wait(dve, l_x[b.par()], b.half(16, 16))
                            wait(dve, s_rstd, (b - 1).count(2, 2))
                            for t in range(TT):
                                dve.bn_stats(bns[:, t, :], xin[:, b.par(), t]).then_inc(s_bn, 1)
                            for t in range(TT):
                                wait(dve, s_bn, b.count(2 * TT, t + 1), alone)
                                dve.bn_aggr(mv[:, t, :], bns[:, t, :]).then_inc(s_bn, 1)
                        if s == AT['n'] and has(3):
                            b = i + 3
                            wait(dve, s_rstd, b.count(2, 2))
                            wait(dve, s_xt, (b - 1).count(1, 1))
                            for t in range(TT):
                                dve.tensor_scalar(xn[:, t], xin[:, b.par(), t], mv[:, t, 0:1], rstd[:, t:t + 1],
                                                  ALU.subtract, ALU.mult).then_inc(s_xn, 1)

                bodies(dve, body)

            @block.tensor
            def _(pe):
                pe.wait_ge(c_pool, n_early)

                def body(i, has):
                    if is_body(i, -1):
                        pe.wait_ge(c_pool, n_early + 2)
                        pe.wait_ge(c_rows, 2)
                    mm = nc.tensor.matmul

                    def scores_max(h):
                        b = i + 1
                        p = b.par()
                        if h % HH == 0:
                            wait(pe, (d_a, d_b)[h // HH][p], b.half(80, 80))
                        wait(pe, s_max, b.count(H, max(0, h - 2)))
                        for t in range(TT):
                            ins = mm(mx_ps[h % 3][:, t, :], Qm[:, p, h, t * P:(t + 1) * P], Kp[:, p, h, :],
                                     start=True, stop=True)
                        ins.then_inc(s_mm, 1)

                    def scores(s):
                        p = i.par()
                        if s == 0:
                            wait(pe, d_m[p], i.half(16, 16))
                        wait(pe, s_exp, i.count(H, s - 1))
                        for t in range(TT):
                            ins = mm(st_ps[s % 2][:, t, :], Kp[:, p, s, t * P:(t + 1) * P], Qp[:, p, s, :],
                                     start=True, stop=True)
                        ins.then_inc(s_st, 1)

                    def values(n, g):
                        b = i + n
                        wait(pe, s_exp, b.count(H, G * g + G))
                        if g == 0:
                            wait(pe, s_vev, b.count(1, 1))
                        wait(pe, s_ou, b.count(NG, g))
                        for t in range(TT):
                            for j in range(G):
                                h = G * g + j
                                ins = mm(pv_ps[32 * j:32 * j + 32, 0:S], V[:, b.par(), t, h, :],
                                         pr[:, h % (2 * G), t, :], start=(t == 0), stop=(t == TT - 1),
                                         tile_position=(0, 32 * j))
                        ins.then_inc(s_pv, 1)

                    def out_transposed(n, k):
                        b = i + n
                        wait(pe, s_ou, b.count(NG, 2 * k + 2))
                        for t in range(TT):
                            for g in range(2):
                                ins = pe.transpose(ms_ps[0][:, t, g * P:(g + 1) * P],
                                                   ou[:, 2 * k + g, t * P:(t + 1) * P], ident[:, :])
                        ins.then_inc(s_at, 1)

                    def project(w16, src, dst, done):
                        for m in range(DC):
                            n = 0
                            for k in range(DC):
                                for pw, px in PASSES:
                                    ins = mm(dst[:, m, :], w16[:, pw, k, m * P:(m + 1) * P], src[:, px, k, :],
                                             start=(n == 0), stop=(n == 5))
                                    n += 1
                        ins.then_inc(done, 1)

                    for s in range(H):
                        if s == AT['x'] and has(2):
                            b = i + 2
                            wait(pe, s_xn, b.count(TT, TT))
                            if has(-1):
                                wait(pe, s_on, (i - 1).count(2, 1))
                            else:
                                wait(pe, s_xlo, (i + 1).count(1, 1))
                            for k in range(DC):
                                for t in range(TT):
                                    ins = pe.transpose(ms_ps[0][:, k, t * P:(t + 1) * P],
                                                       xn[:, t, k * P:(k + 1) * P], ident[:, :])
                            ins.then_inc(s_xt, 1)
                        if s == AT['q'] and has(2):
                            b = i + 2
                            wait(pe, s_xlo, b.count(1, 1))
                            if has(0):
                                wait(pe, s_vev, i.count(1, 1))
                            else:
                                wait(pe, s_klo, (i + 1).count(1, 1))
                            if is_body(i, -2):
                                pe.wait_ge(c_dve, n_dve)
                            project(wq16, xT, ms_ps[1], s_q)
                        if s == AT['a1'] and has(-1):
                            if has(2):
                                wait(pe, s_xlo, (i + 2).count(1, 1))
                            else:
                                wait(pe, s_on, (i - 1).count(2, 1))
                            out_transposed(-1, 1)
                        if s == AT['k'] and has(2):
                            b = i + 2
                            wait(pe, s_ct, b.count(2, 2))
                            wait(pe, s_qlo, b.count(1, 1))
                            project(wk16, cT[:, b.par()], ms_ps[1], s_k)
                        if s == AT['b'] and has(-1):
                            b = i - 1
                            wait(pe, s_on, b.count(2, 2))
                            for k in range(DC):
                                for t in range(TT):
                                    ins = pe.transpose(ms_ps[0][:, k, t * P:(t + 1) * P],
                                                       on[:, t, k * P:(k + 1) * P], ident[:, :])
                            ins.then_inc(s_bt, 1)
                        if s == AT['o'] and has(-1):
                            b = i - 1
                            wait(pe, s_olo, b.count(1, 1))
                            for t in range(TT):
                                n = 0
                                for k in range(DC):
                                    for pw, px in PASSES:
                                        ins = mm(ms_ps[0][:, t, :], oT[:, px, k, t * P:(t + 1) * P],
                                                 wo16[:, pw, k, :], start=(n == 0), stop=(n == 5))
                                        n += 1
                            ins.then_inc(s_o, 1)
                        if s == AT['m'] and has(1):
                            b = i + 1
                            wait(pe, s_max, b.count(H, H))
                            if has(2):
                                wait(pe, s_klo, (i + 2).count(1, 1))
                            else:
                                wait(pe, s_vev, i.count(1, 1))
                            for t in range(TT):
                                ins = pe.transpose(ms_ps[1][0:H, 0, t * P:(t + 1) * P], mx[:, b.par(), t, :],
                                                   ident[:, :])
                            ins.then_inc(s_mt, 1)
                        if s == AT['a0'] and has(0):
                            if has(-1):
                                wait(pe, s_res, (i - 1).count(TT, TT))
                            else:
                                wait(pe, s_xlo, (i + 2).count(1, 1))
                            out_transposed(0, 0)
                        if s == AT['v'] and has(1):
                            b = i + 1
                            wait(pe, s_mrow, b.count(1, 1))
                            for t in range(TT):
                                n = 0
                                for k in range(DC):
                                    for pw, px in PASSES:
                                        ins = mm(ms_ps[1][:, t, :], cT[:, b.par(), px, k, t * P:(t + 1) * P],
                                                 wv16[:, pw, k, :], start=(n == 0), stop=(n == 5 and not bias))
                                        n += 1
                                if bias:
                                    for part in range(2):
                                        ins = mm(ms_ps[1][:, t, :], ones16[:, :], bv16[:, part, :],
                                                 start=False, stop=(part == 1))
                            ins.then_inc(s_v, 1)
                        if has(1):
                            for h in max_slots(s):
                                scores_max(h)
                        if has(0):
                            scores(s)
                        n, g = grouped(s, AT['p'])
                        if g is not None and has(n):
                            values(n, g)

                bodies(pe, body)

        clear(nc, sems)


TM = 512
TQ = TM // P
NE = 8
FE = 512
FT = 1024


def ternary_mlp(nc, tag, NT, x_in, w_upT, w_downT, gate, x_out):
    NF = FT // P
    x_t = x_in.rearrange("(b t p) d -> b p t d", t=TQ, p=P)
    o_t = x_out.rearrange("(b t p) d -> b p t d", t=TQ, p=P)
    sems = []
    with ExitStack() as ctx:
        def sb(name, shape, dt):
            return ctx.enter_context(nc.sbuf_tensor(f"{tag}_{name}", shape, dt))

        def pb(name, shape, dt):
            return ctx.enter_context(nc.psum_tensor(f"{tag}_{name}", shape, dt))

        def sem(name):
            sems.append(ctx.enter_context(nc.semaphore(f"{tag}_{name}")))
            return sems[-1]

        wu32 = sb("wu32", [P, DC * FT], F32)
        wd32 = sb("wd32", [P, NF * D], F32)
        wneg = sb("wneg", [P, DC * FT], F16)
        wu16 = sb("wu16", [P, DC, FT], F16)
        wd16 = sb("wd16", [P, NF, D], F16)
        wsum = sb("wsum", [P, 2], F32)
        thr = sb("thr", [P, 4], F32)
        ident = sb("ident", [P, P], F32)
        ones = sb("ones", [P, P], F32)
        expo = sb("expo", [P, 2, TQ], F32)
        tg = sb("tg", [P, 1], F32)
        xin = sb("xin", [P, 2, TQ, D], F32)
        xres = sb("xres", [P, 2, TQ, D], F32)
        bns = sb("bns", [P, TQ, 6], F32)
        mv = sb("mv", [P, TQ, 2], F32)
        vpe = sb("vpe", [P, TQ], F32)
        rstd = sb("rstd", [P, TQ], F32)
        sd = sb("sd", [P, TQ], F32)
        den = sb("den", [P, TQ], F32)
        rden = sb("rden", [P, TQ], F32)
        scl = sb("scl", [P, TQ], F32)
        xn = sb("xn", [P, TQ, D], F32)
        xT = sb("xT", [P, 2, 2, DC, TM], F16)
        h32 = sb("h32", [P, 2, TM], F32)
        hsq = sb("hsq", [P, 2, TM], F32)
        hT = sb("hT", [P, 2, 2, NF, TM], F16)
        ssq = sb("ssq", [P, 2, TM], F32)
        msq = sb("msq", [P, TQ], F32)
        rms = sb("rms", [P, TQ], F32)
        rinv = sb("rinv", [P, TQ], F32)
        oscl = sb("oscl", [P, TQ], F32)

        t_ps = [pb(f"t_ps{i}", [P, TM], F32) for i in range(DC)]
        u_ps = [pb(f"u_ps{i}", [P, TM], F32) for i in range(3)]
        d_ps = [pb(f"d_ps{i}", [P, 2, D], F32) for i in range(2)]
        s_ps = pb("s_ps", [P, TQ], F32)

        alone = sem("alone")
        l_w = sem("l_w")
        c_pool = sem("c_pool")
        c_dve = sem("c_dve")
        c_sum = sem("c_sum")
        c_tanh = sem("c_tanh")
        l_x = [sem(f"l_x{i}") for i in range(2)]
        l_r = [sem(f"l_r{i}") for i in range(2)]
        st_o = [sem(f"st_o{i}") for i in range(2)]
        s_bn = sem("s_bn")
        s_pow = sem("s_pow")
        s_scl = sem("s_scl")
        s_xn = sem("s_xn")
        s_xt = sem("s_xt")
        s_xhi = sem("s_xhi")
        s_xlo = sem("s_xlo")
        s_u = sem("s_u")
        s_h = sem("s_h")
        s_sq = sem("s_sq")
        s_hhi = sem("s_hhi")
        s_hlo = sem("s_hlo")
        s_acc = sem("s_acc")
        s_ms = sem("s_ms")
        s_msq = sem("s_msq")
        s_rms = sem("s_rms")
        s_os = sem("s_os")
        s_d = sem("s_d")
        s_res = sem("s_res")

        AT = dict(ms=2, mean=2, rms=3, scale=3, o0=4, o1=7, x=3, hi=3, lo=4, stat=2, var=4, norm=7)
        LOOP = (3, NT - 3)

        def bodies(eng, body):
            for c in range(-2, LOOP[0]):
                body(At(None, c), lambda n, c=c: 0 <= c + n < NT)
            with eng.Fori(0, (LOOP[1] - LOOP[0]) // 2) as it:
                for u in range(2):
                    body(At(it, LOOP[0] + u), lambda n: True)
            for c in range(LOOP[1], NT + 1):
                body(At(None, c), lambda n, c=c: 0 <= c + n < NT)

        with nc.Block() as block:

            @block.sync
            def _(sp):
                def body(i, has):
                    if has(2):
                        b = i + 2
                        wait(sp, s_xn, (b - 2).count(TQ, TQ), alone)
                        sp.dma_start(xin[:, b.par()], x_t[b.index()]).then_inc(l_x[b.par()], 16)
                    if is_body(i, -2):
                        sp.dma_start(wu32[:, :].rearrange("p (k n) -> p k n", k=DC),
                                     w_upT.rearrange("(k p) n -> p k n", p=P)).then_inc(l_w, 16)
                        sp.dma_start(wd32[:, :].rearrange("p (k n) -> p k n", k=NF),
                                     w_downT.rearrange("(k p) n -> p k n", p=P)).then_inc(l_w, 16)
                        sp.dma_start(tg[:, :], gate.rearrange("(a n) -> a n", a=1).broadcast_to([P, 1])).then_inc(l_w, 16)
                    if has(0):
                        wait(sp, st_o[i.par()], (i - 2).half(16, 16), alone)
                        sp.dma_start(xres[:, i.par()], x_t[i.index()]).then_inc(l_r[i.par()], 16)
                    if has(-1):
                        b = i - 1
                        wait(sp, s_res, b.count(TQ, TQ), alone)
                        sp.dma_start(o_t[b.index()], xres[:, b.par()]).then_inc(st_o[b.par()], 16)

                bodies(sp, body)
                for p in range(2):
                    sp.wait_ge(st_o[p], 16 * (NT // 2))

            @block.gpsimd
            def _(pool):
                pool.memset(ident[:, :], 0.0).then_inc(c_pool, 1)
                pool.memset(ones[:, :], 1.0).then_inc(c_pool, 1)
                pool.memset(expo[:, 0, :], -0.5).then_inc(c_pool, 1)
                pool.memset(expo[:, 1, :], 0.5).then_inc(c_pool, 1)
                pool.wait_ge(c_pool, 4)
                pool.affine_select(out=ident[:, :], in_=ident[:, :], compare_op=ALU.not_equal, fill=1.0,
                                   base=0, pattern=[[-1, P]], channel_multiplier=1).then_inc(c_pool, 1)

                def body(i, has):
                    def rms_of_h(b):
                        wait(pool, s_msq, b.count(1, 1), alone)
                        wait(pool, s_os, (b - 1).count(3, 1), alone)
                        pool.tensor_tensor(rms[:, :], msq[:, :], expo[:, 1, :], ALU.pow).then_inc(s_rms, 1)

                    if has(-1) and not has(0):
                        rms_of_h(i - 1)
                    if has(0):
                        for f in range(NF):
                            if f == AT['rms'] and has(-1):
                                rms_of_h(i - 1)
                            wait(pool, s_sq, i.count(NF, f + 1), alone)
                            if f == 0:
                                wait(pool, s_ms, (i - 2).count(1, 1), alone)
                                pool.tensor_scalar(ssq[:, i.par()], hsq[:, f % 2], 1.0, None,
                                                   ALU.mult).then_inc(s_acc, 1)
                            else:
                                wait(pool, s_acc, i.count(NF, f), alone)
                                pool.tensor_tensor(ssq[:, i.par()], ssq[:, i.par()], hsq[:, f % 2],
                                                   ALU.add).then_inc(s_acc, 1)
                            if f == AT['var'] and has(2):
                                variances(i + 2)
                    elif has(2):
                        variances(i + 2)

                def variances(b):
                    wait(pool, s_bn, b.count(2 * TQ, 2 * TQ), alone)
                    wait(pool, s_scl, (b - 1).count(4, 4), alone)
                    pool.tensor_scalar(vpe[:, :], mv[:, :, 1], EPS, None, ALU.add).then_inc(s_pow, 1)
                    pool.tensor_tensor(sd[:, :], mv[:, :, 1], expo[:, 1, :], ALU.pow).then_inc(s_pow, 1)
                    wait(pool, s_pow, b.count(3, 2), alone)
                    pool.tensor_tensor(rstd[:, :], vpe[:, :], expo[:, 0, :], ALU.pow).then_inc(s_pow, 1)

                bodies(pool, body)

            @block.scalar
            def _(act):
                act.wait_ge(l_w, 48)
                act.activation(tg[:, :], tg[:, :], ACT.Tanh).then_inc(c_tanh, 1)

                def body(i, has):
                    def x_hi():
                        b = i + 1
                        wait(act, s_u, (b - 2).count(NF, NF))
                        for k in range(DC):
                            wait(act, s_xt, b.count(DC, k + 1))
                            act.activation(xT[:, b.par(), HI, k], t_ps[k][:, :], ACT.Identity).then_inc(s_xhi, 1)

                    for f in range(NF):
                        if has(0):
                            wait(act, s_u, i.count(NF, f + 1))
                            wait(act, s_sq, i.count(NF, f - 1))
                            wait(act, s_hlo, i.count(NF, f - 1))
                            act.activation(h32[:, f % 2], u_ps[f % 3][:, :], ACT.Gelu).then_inc(s_h, 1)
                            wait(act, s_h, i.count(NF, f + 1))
                            wait(act, s_acc, i.count(NF, f - 1))
                            act.activation(hsq[:, f % 2], h32[:, f % 2], ACT.Square).then_inc(s_sq, 1)
                        if f == AT['hi'] and has(1):
                            x_hi()

                bodies(act, body)

            @block.vector
            def _(dve):
                def thresholds():
                    dve.wait_ge(l_w, 48)
                    for j, w in enumerate((wu32, wd32)):
                        dve.tensor_reduce(wsum[:, j:j + 1], w[:, :], AX_X, ALU.add,
                                          apply_absolute_value=True).then_inc(c_dve, 1)
                    dve.wait_ge(c_sum, 1)
                    dve.tensor_scalar(thr[:, 0:2], s_ps[:, 0:2], 0.5 / (D * FT), None, ALU.mult).then_inc(c_dve, 1)
                    dve.tensor_scalar(thr[:, 2:4], s_ps[:, 0:2], -0.5 / (D * FT), None, ALU.mult).then_inc(c_dve, 1)
                    dve.wait_ge(c_dve, 4)

                def ternary(j, w, w16):
                    n = 4 + 2 * j
                    dve.tensor_scalar(wneg[:, :], w[:, :], thr[:, 2 + j:3 + j], None, ALU.is_lt).then_inc(c_dve, 1)
                    dve.wait_ge(c_dve, n + 1)
                    dve.scalar_tensor_tensor(w16[:, :, :].rearrange("p k n -> p (k n)"), w[:, :], thr[:, j:j + 1],
                                             wneg[:, :], ALU.is_gt, ALU.subtract).then_inc(c_dve, 1)
                    dve.wait_ge(c_dve, n + 2)

                def statistics(b):
                    wait(dve, l_x[b.par()], b.half(16, 16))
                    wait(dve, s_xn, (b - 1).count(TQ, TQ))
                    for t in range(TQ):
                        dve.bn_stats(bns[:, t, :], xin[:, b.par(), t]).then_inc(s_bn, 1)
                    for t in range(TQ):
                        wait(dve, s_bn, b.count(2 * TQ, t + 1), alone)
                        dve.bn_aggr(mv[:, t, :], bns[:, t, :]).then_inc(s_bn, 1)

                def normalise(b):
                    wait(dve, s_pow, b.count(3, 3))
                    dve.tensor_tensor(den[:, :], sd[:, :], rstd[:, :], ALU.mult).then_inc(s_scl, 1)
                    wait(dve, s_scl, b.count(4, 1))
                    dve.tensor_scalar(den[:, :], den[:, :], 1e-8, None, ALU.add).then_inc(s_scl, 1)
                    wait(dve, s_scl, b.count(4, 2))
                    dve.reciprocal(rden[:, :], den[:, :]).then_inc(s_scl, 1)
                    wait(dve, s_scl, b.count(4, 3))
                    dve.tensor_tensor(scl[:, :], rden[:, :], rstd[:, :], ALU.mult).then_inc(s_scl, 1)
                    wait(dve, s_scl, b.count(4, 4))
                    wait(dve, s_xt, (b - 1).count(DC, DC))
                    for t in range(TQ):
                        dve.tensor_scalar(xn[:, t], xin[:, b.par(), t], mv[:, t, 0:1], scl[:, t:t + 1],
                                          ALU.subtract, ALU.mult).then_inc(s_xn, 1)

                def body(i, has):
                    if is_body(i, -1):
                        thresholds()
                        ternary(0, wu32, wu16)
                    if is_body(i, 0):
                        ternary(1, wd32, wd16)
                        dve.wait_ge(c_tanh, 1)
                    for f in range(NF):
                        if has(0):
                            n = i.count(NF, f + 1)
                            wait(dve, s_h, n)
                            if f == 0:
                                wait(dve, s_d, (i - 2).count(2, 2))
                            dve.tensor_copy(hT[:, i.par(), HI, f], h32[:, f % 2]).then_inc(s_hhi, 1)
                            wait(dve, s_hhi, n)
                            dve.tensor_tensor(hT[:, i.par(), LO, f], h32[:, f % 2], hT[:, i.par(), HI, f],
                                              ALU.subtract).then_inc(s_hlo, 1)
                        if f == AT['mean'] and has(-1):
                            b = i - 1
                            wait(dve, s_ms, b.count(1, 1))
                            dve.tensor_scalar(msq[:, :], s_ps[:, :], 1.0 / FT, None, ALU.mult).then_inc(s_msq, 1)
                        if f == AT['scale'] and has(-1):
                            b = i - 1
                            wait(dve, s_rms, b.count(1, 1))
                            dve.tensor_scalar(oscl[:, :], rms[:, :], 1e-8, None, ALU.add).then_inc(s_os, 1)
                            wait(dve, s_os, b.count(3, 1))
                            dve.reciprocal(rinv[:, :], oscl[:, :]).then_inc(s_os, 1)
                            wait(dve, s_os, b.count(3, 2))
                            dve.tensor_scalar(oscl[:, :], rinv[:, :], tg[:, 0:1], None, ALU.mult).then_inc(s_os, 1)
                            wait(dve, s_os, b.count(3, 3))
                        if f == AT['lo'] and has(1):
                            b = i + 1
                            for k in range(DC):
                                wait(dve, s_xhi, b.count(DC, k + 1))
                                dve.tensor_tensor(xT[:, b.par(), LO, k], t_ps[k][:, :], xT[:, b.par(), HI, k],
                                                  ALU.subtract).then_inc(s_xlo, 1)
                        if f in (AT['o0'], AT['o1']) and has(-1):
                            b = i - 1
                            k = 0 if f == AT['o0'] else 1
                            wait(dve, s_d, b.count(2, k + 1))
                            wait(dve, l_r[b.par()], b.half(16, 16))
                            for t in (2 * k, 2 * k + 1):
                                dve.scalar_tensor_tensor(xres[:, b.par(), t], d_ps[k][:, t % 2, :],
                                                         oscl[:, t:t + 1], xres[:, b.par(), t],
                                                         ALU.mult, ALU.add).then_inc(s_res, 1)
                        if f == AT['stat'] and has(2):
                            statistics(i + 2)
                        if f == AT['norm'] and has(2):
                            normalise(i + 2)

                bodies(dve, body)

            @block.tensor
            def _(pe):
                mm = nc.tensor.matmul
                pe.wait_ge(c_dve, 2)
                pe.wait_ge(c_pool, 5)
                mm(s_ps[:, 0:2], ones[:, :], wsum[:, :], start=True, stop=True).then_inc(c_sum, 1)

                def down(b, t):
                    n = 0
                    for f in range(NF):
                        for part in range(2):
                            ins = mm(d_ps[t // 2][:, t % 2, :], hT[:, b.par(), part, f, t * P:(t + 1) * P],
                                     wd16[:, f, :], start=(n == 0), stop=(n == 2 * NF - 1))
                            n += 1
                    if t % 2:
                        ins.then_inc(s_d, 1)

                def body(i, has):
                    if is_body(i, 0):
                        pe.wait_ge(c_dve, 6)
                    if is_body(i, 1):
                        pe.wait_ge(c_dve, 8)
                    for f in range(NF):
                        if has(0):
                            if f == 0:
                                wait(pe, s_xlo, i.count(DC, DC))
                            wait(pe, s_h, i.count(NF, f - 1 if f < 2 else max(0, f - 2)))
                            n = 0
                            for k in range(DC):
                                for part in range(2):
                                    ins = mm(u_ps[f % 3][:, :], wu16[:, k, f * P:(f + 1) * P], xT[:, i.par(), part, k, :],
                                             start=(n == 0), stop=(n == 3))
                                    n += 1
                            ins.then_inc(s_u, 1)
                        if f == AT['ms'] and has(-1):
                            b = i - 1
                            wait(pe, s_acc, b.count(NF, NF))
                            wait(pe, s_msq, (b - 1).count(1, 1))
                            for t in range(TQ):
                                ins = mm(s_ps[:, t:t + 1], ssq[:, b.par(), t * P:(t + 1) * P], ones[:, 0:1],
                                         start=True, stop=True)
                            ins.then_inc(s_ms, 1)
                        if f % 2 and has(-1):
                            b = i - 1
                            t = f // 2
                            if t == 0:
                                wait(pe, s_hlo, b.count(NF, NF))
                            if t % 2 == 0:
                                wait(pe, s_res, (b - 1).count(TQ, t + 2))
                            down(b, t)
                        if f == AT['x'] and has(1):
                            b = i + 1
                            wait(pe, s_xn, b.count(TQ, TQ))
                            wait(pe, s_xlo, (b - 1).count(DC, DC))
                            for k in range(DC):
                                for t in range(TQ):
                                    ins = pe.transpose(t_ps[k][:, t * P:(t + 1) * P],
                                                       xn[:, t, k * P:(k + 1) * P], ident[:, :])
                                ins.then_inc(s_xt, 1)

                bodies(pe, body)

        clear(nc, sems)


def moe(nc, tag, NT, x_in, wg, wu, wd, w1, w2, gate, out):
    T = NT * TM
    NC = T // P
    NTE = 2 * T // TM + NE - 1
    NS = NTE * TM
    NF = FE // P
    PAD = 1 << 20
    WN = DC * FE
    x_t = x_in.rearrange("(b t p) d -> b p t d", t=TQ, p=P)
    o_t = out.rearrange("(b t p) d -> b p t d", t=TQ, p=P)
    wu_e = wu.rearrange("e (k p) n -> e p k n", p=P)
    wd_e = wd.rearrange("e (k p) n -> e p k n", p=P)
    xn_d = nc.dram_tensor(f"{tag}_xn_dram", (T, D), F32, kind="Internal").ap()
    xn_t = xn_d.rearrange("(b t p) d -> b p t d", t=TQ, p=P)
    table = nc.dram_tensor(f"{tag}_table", (NS, 2), I32, kind="Internal").ap()
    table_t = table.rearrange("(b t p) w -> b p t w", t=TQ, p=P)

    sems = []
    with ExitStack() as ctx:
        def sb(name, shape, dt, c=ctx):
            return c.enter_context(nc.sbuf_tensor(f"{tag}_{name}", shape, dt))

        def pb(name, shape, dt, c=ctx):
            return c.enter_context(nc.psum_tensor(f"{tag}_{name}", shape, dt))

        def sem(name):
            sems.append(ctx.enter_context(nc.semaphore(f"{tag}_{name}")))
            return sems[-1]

        def loop_bodies(eng, body, first, lo, hi, n):
            for c in range(first, lo):
                body(At(None, c), lambda k, c=c: 0 <= c + k < n)
            with eng.Fori(0, (hi - lo) // 2) as it:
                for u in range(2):
                    body(At(it, lo + u), lambda k: True)
            for c in range(hi, n + 1):
                body(At(None, c), lambda k, c=c: 0 <= c + k < n)

        ident = sb("ident", [P, P], F32)
        tg = sb("tg", [P, 1], F32)
        te = sb("te", [1, NTE + 1], I32)
        alone = sem("alone")
        c_pool = sem("c_pool")

        wu_all = sb("wu_all", [P, 2, NE * WN], F16)
        wd_all = sb("wd_all", [P, 2, NE * WN], F16)

        early = ctx.enter_context(ExitStack())
        xall = sb("xall", [P, 2, DC, T], F16, early)
        lg = sb("lg", [P, NC, NE], F32, early)
        pair = sb("pair", [P, NC, 2, 2], I32, early)
        slot = sb("slot", [P, NC, 2], I32, early)
        s1 = sb("s1", [P, 2, DC, FE], F16, early)
        s2 = sb("s2", [P, 2, NF, D], F16, early)
        tgs = sb("tgs", [P, 1], F32, early)

        with ExitStack() as c1:
            wgl = sb("wgl", [P, DC, NE], F32, c1)
            wg16 = sb("wg16", [P, 2, DC, NE], F16, c1)
            half_neg = sb("half_neg", [P, TQ], F32, c1)
            pads = sb("pads", [P, NS // P, 2], I32, c1)
            xin = sb("xin", [P, 2, TQ, D], F32, c1)
            bns = sb("bns", [P, TQ, 6], F32, c1)
            mv = sb("mv", [P, TQ, 2], F32, c1)
            vpe = sb("vpe", [P, TQ], F32, c1)
            rstd = sb("rstd", [P, TQ], F32, c1)
            xn = sb("xn", [P, 2, TQ, D], F32, c1)
            w32 = sb("w32", [P, 2, WN], F32, c1)
            s32 = sb("s32", [P, 2, WN], F32, c1)
            t_ps = [[pb(f"rt_ps{i}{k}", [P, TM], F32, c1) for k in range(DC)] for i in range(2)]
            l_ps = [pb(f"l_ps{i}", [P, TQ, NE], F32, c1) for i in range(2)]
            l_w = sem("l_w")
            l_s = sem("l_s")
            c_tanh = sem("c_tanh")
            c_dve = sem("c_dve")
            l_x = [sem(f"rl_x{i}") for i in range(2)]
            l_e = [sem(f"rl_e{i}") for i in range(2)]
            st_n = [sem(f"st_n{i}") for i in range(2)]
            st_t = sem("st_t")
            s_bn = sem("r_bn")
            s_rstd = sem("r_rstd")
            s_xn = sem("r_xn")
            s_xt = sem("r_xt")
            s_xhi = sem("r_xhi")
            s_xlo = sem("r_xlo")
            s_l = sem("r_l")
            s_lg = sem("r_lg")
            s_whi = sem("r_whi")
            s_wlo = sem("r_wlo")
            assert NT == 2 * NE

            def bodies(eng, body):
                loop_bodies(eng, body, -2, 2, NT - 2, NT)

            def job(b):
                src, dst = ((wu_e, wu_all), (wd_e, wd_all))[b.par()]
                e = b.c // 2 if b.it is None else b.it + b.c // 2
                return src[e], [dst[:, part, bass.ds(e * WN, WN)] for part in range(2)]

            with nc.Block() as block:
                @block.sync
                def _(sp):
                    sp.dma_start(wgl[:, :, :], wg.rearrange("(k p) n -> p k n", p=P)).then_inc(l_w, 16)
                    sp.dma_start(tg[:, :], gate.rearrange("(a n) -> a n", a=1).broadcast_to([P, 1])).then_inc(l_w, 16)
                    sp.wait_ge(c_pool, 5)
                    sp.dma_start(table.rearrange("(p n) w -> p n w", p=P), pads[:, :, :]).then_inc(st_t, 16)

                    def body(i, has):
                        if has(2):
                            b = i + 2
                            wait(sp, s_xn, (b - 2).count(TQ, TQ), alone)
                            sp.dma_start(xin[:, b.par()], x_t[b.index()]).then_inc(l_x[b.par()], 16)
                        if has(1):
                            b = i + 1
                            src = job(b)[0]
                            wait(sp, s_wlo, (b - 2).count(1, 1), alone)
                            sp.dma_start(w32[:, b.par()].rearrange("p (k n) -> p k n", k=src.shape[1]),
                                         src).then_inc(l_e[b.par()], 16)
                            wait(sp, s_xn, b.count(TQ, TQ), alone)
                            sp.dma_start(xn_t[b.index()], xn[:, b.par()]).then_inc(st_n[b.par()], 16)

                        if is_body(i, -1):
                            sp.dma_start(s32[:, 0].rearrange("p (k n) -> p k n", k=DC),
                                         w1.rearrange("(k p) n -> p k n", p=P)).then_inc(l_s, 16)
                            sp.dma_start(s32[:, 1].rearrange("p (k n) -> p k n", k=NF),
                                         w2.rearrange("(k p) n -> p k n", p=P)).then_inc(l_s, 16)

                    bodies(sp, body)
                    sp.wait_ge(st_t, 16)
                    for p in range(2):
                        sp.wait_ge(st_n[p], 16 * (NT // 2))

                @block.gpsimd
                def _(pool):
                    pool.memset(ident[:, :], 0.0).then_inc(c_pool, 1)
                    pool.memset(half_neg[:, :], -0.5).then_inc(c_pool, 1)
                    pool.memset(pads[:, :, :], PAD).then_inc(c_pool, 1)
                    pool.wait_ge(c_pool, 3)
                    pool.affine_select(out=ident[:, :], in_=ident[:, :], compare_op=ALU.not_equal, fill=1.0,
                                       base=0, pattern=[[-1, P]], channel_multiplier=1).then_inc(c_pool, 1)
                    pool.memset(pads[:, :, 1], 0).then_inc(c_pool, 1)

                    def body(i, has):
                        if has(0):
                            wait(pool, s_whi, i.count(2, 2), alone)
                            hi, lo = job(i)[1]
                            pool.tensor_tensor(lo, w32[:, i.par()], hi,
                                               ALU.subtract).then_inc(s_wlo, 1)
                        if has(2):
                            b = i + 2
                            wait(pool, s_bn, b.count(2 * TQ, 2 * TQ), alone)
                            wait(pool, s_xn, (b - 1).count(TQ, TQ), alone)
                            pool.tensor_scalar(vpe[:, :], mv[:, :, 1], EPS, None, ALU.add).then_inc(s_rstd, 1)
                            wait(pool, s_rstd, b.count(2, 1), alone)
                            pool.tensor_tensor(rstd[:, :], vpe[:, :], half_neg[:, :], ALU.pow).then_inc(s_rstd, 1)

                    bodies(pool, body)
                    for c in range(2):
                        pool.iota(pair[:, :, c, 0], pattern=[[P, NC]], base=0, channel_multiplier=1)\
                            .then_inc(c_pool, 1)

                @block.scalar
                def _(act):
                    act.wait_ge(l_w, 32)
                    act.activation(tg[:, :], tg[:, :], ACT.Tanh).then_inc(c_tanh, 1)

                    def body(i, has):
                        if has(0):
                            for k in range(DC):
                                wait(act, s_xt, i.count(DC, k + 1))
                                act.activation(xall[:, HI, k, bass.ds(i.index() * TM, TM)],
                                               t_ps[i.par()][k][:, :], ACT.Identity).then_inc(s_xhi, 1)
                            wait(act, l_e[i.par()], i.half(16, 16))
                            act.activation(w32[:, i.par()], w32[:, i.par()], ACT.Identity,
                                           scale=WS).then_inc(s_whi, 1)
                            wait(act, s_whi, i.count(2, 1))
                            act.activation(job(i)[1][HI], w32[:, i.par()], ACT.Identity).then_inc(s_whi, 1)

                    bodies(act, body)

                @block.vector
                def _(dve):
                    dve.wait_ge(l_w, 32)
                    split_weight(dve, c_dve, 0, wgl[:, :, :], wg16, WS)
                    dve.wait_ge(c_dve, 3)

                    def body(i, has):
                        if has(0):
                            for k in range(DC):
                                wait(dve, s_xhi, i.count(DC, k + 1))
                                cols = bass.ds(i.index() * TM, TM)
                                dve.tensor_tensor(xall[:, LO, k, cols], t_ps[i.par()][k][:, :],
                                                  xall[:, HI, k, cols], ALU.subtract).then_inc(s_xlo, 1)
                        if has(1):
                            b = i + 1
                            wait(dve, s_rstd, b.count(2, 2))
                            wait(dve, s_xt, (b - 2).count(DC, DC))
                            wait(dve, st_n[b.par()], (b - 2).half(16, 16))
                            for t in range(TQ):
                                dve.tensor_scalar(xn[:, b.par(), t], xin[:, b.par(), t], mv[:, t, 0:1],
                                                  rstd[:, t:t + 1], ALU.subtract, ALU.mult).then_inc(s_xn, 1)
                        if has(-1):
                            b = i - 1
                            wait(dve, s_l, b.count(1, 1))
                            dve.tensor_scalar(lg[:, bass.ds(b.index() * TQ, TQ), :], l_ps[b.par()][:, :, :],
                                              1.0 / WS, None, ALU.mult).then_inc(s_lg, 1)
                        if has(2):
                            b = i + 2
                            wait(dve, l_x[b.par()], b.half(16, 16))
                            wait(dve, s_rstd, (b - 1).count(2, 1))
                            for t in range(TQ):
                                dve.bn_stats(bns[:, t, :], xin[:, b.par(), t]).then_inc(s_bn, 1)
                            for t in range(TQ):
                                wait(dve, s_bn, b.count(2 * TQ, t + 1), alone)
                                dve.bn_aggr(mv[:, t, :], bns[:, t, :]).then_inc(s_bn, 1)

                    bodies(dve, body)
                    dve.wait_ge(l_s, 32)
                    n = split_weight(dve, c_dve, 3, s32[:, 0], s1.ap().rearrange("p a k n -> p a (k n)"), WS)
                    n = split_weight(dve, c_dve, n, s32[:, 1], s2.ap().rearrange("p a k n -> p a (k n)"), WS)
                    dve.wait_ge(c_tanh, 1)
                    dve.tensor_scalar(tgs[:, :], tg[:, :], 1.0 / WS, None, ALU.mult).then_inc(c_dve, 1)
                    dve.wait_ge(c_dve, n + 1)

                @block.tensor
                def _(pe):
                    mm = nc.tensor.matmul
                    pe.wait_ge(c_pool, 4)
                    pe.wait_ge(c_dve, 3)

                    def body(i, has):
                        if has(1):
                            b = i + 1
                            wait(pe, s_xn, b.count(TQ, TQ))
                            wait(pe, s_xlo, (b - 2).count(DC, DC))
                            for k in range(DC):
                                for t in range(TQ):
                                    ins = pe.transpose(t_ps[b.par()][k][:, t * P:(t + 1) * P],
                                                       xn[:, b.par(), t, k * P:(k + 1) * P], ident[:, :])
                                ins.then_inc(s_xt, 1)
                        if has(0):
                            wait(pe, s_xlo, i.count(DC, DC))
                            wait(pe, s_lg, (i - 2).count(1, 1))
                            for t in range(TQ):
                                n = 0
                                for k in range(DC):
                                    for pw, px in PASSES:
                                        ins = mm(l_ps[i.par()][:, t, :],
                                                 xall[:, px, k, bass.ds(i.index() * TM + t * P, P)],
                                                 wg16[:, pw, k, :], start=(n == 0), stop=(n == 5))
                                        n += 1
                            ins.then_inc(s_l, 1)

                    bodies(pe, body)

        with ExitStack() as c3:
            xres = sb("xres", [P, 2, TQ, D], F32, c3)
            h32 = sb("h32", [P, 2, TM], F32, c3)
            hT = sb("hT", [P, 2, 2, NF, TM], F16, c3)
            PUT = 4
            idx = sb("idx", [P, 2, PUT, 2], I32, c3)
            ent = sb("ent", [P, 2, PUT, 2, 2], I32, c3)

            def arr(name):
                return sb(name, [P, NC, NE], F32, c3)

            ie = arr("ie")
            eq = arr("eq")
            oh = [arr("oh1"), arr("oh2")]
            l2 = arr("l2")
            hot16 = sb("hot16", [P, NC, NE], F16, c3)
            below = sb("below", [P, P], F16, c3)
            ones16 = sb("ones16", [P, P], F16, c3)
            cum = [arr("cum0"), arr("cum1")]
            tot = arr("tot")
            pos = arr("pos")
            tmp = arr("tmp")
            m = [sb(f"m{i}", [P, NC], F32, c3) for i in range(2)]
            sc = [sb(f"sc{i}", [P, NC], F32, c3) for i in range(2)]
            ex = sb("ex", [P, NC], F32, c3)
            dn = sb("dn", [P, NC], F32, c3)
            w = [sb(f"w{i}", [P, NC], F32, c3) for i in range(2)]
            cnt = sb("cnt", [P, NE], F32, c3)
            cnti = sb("cnti", [P, NE], I32, c3)
            tiles = [sb(f"tiles{i}", [P, NE], F32, c3) for i in range(2)]
            ntile = sb("ntile", [P, NE], F32, c3)
            tid = sb("tid", [1, NTE + 1, NE], F32, c3)
            tcmp = sb("tcmp", [1, NTE + 1, NE], F32, c3)
            tef = sb("tef", [1, NTE + 1], F32, c3)
            z_ps = [pb(f"z_ps{i}", [P, NC * NE], F32, c3) for i in range(2)]
            q_pool = sem("q_pool")
            q_pe = sem("q_pe")
            q_act = sem("q_act")
            q_dve = sem("q_dve")
            at = {}
            LEVELS = NC.bit_length() - 1
            PEEL = 4
            ROUTED = 13 + 5 + 1 + 2 * LEVELS + (8 + 2 * (NE.bit_length() - 1)) + 5 + 6
            u_ps = [pb(f"su_ps{i}", [P, TM], F32, c3) for i in range(3)]
            d_ps = [pb(f"sd_ps{i}", [P, 2, D], F32, c3) for i in range(2)]
            l_r = [sem(f"h_lr{i}") for i in range(2)]
            st_o = [sem(f"h_st{i}") for i in range(2)]
            s_u = sem("h_u")
            s_h = sem("h_h")
            s_hhi = sem("h_hhi")
            s_hlo = sem("h_hlo")
            s_d = sem("h_d")
            s_res = sem("h_res")
            g_copy = sem("g_copy")
            g_put = [sem(f"g_put{i}") for i in range(2)]

            assert LEVELS % 2 == 0 and (8 + LEVELS // 2) // NF < PEEL

            def bodies(eng, body):
                loop_bodies(eng, body, 0, PEEL, NT, NT)

            with nc.Block() as block:
                @block.sync
                def _(sp):
                    def body(i, has):
                        if has(0):
                            wait(sp, st_o[i.par()], (i - 2).half(16, 16), alone)
                            sp.dma_start(xres[:, i.par()], x_t[i.index()]).then_inc(l_r[i.par()], 16)
                        if has(-1):
                            b = i - 1
                            wait(sp, s_res, b.count(TQ, TQ), alone)
                            sp.dma_start(o_t[b.index()], xres[:, b.par()]).then_inc(st_o[b.par()], 16)

                    bodies(sp, body)
                    for p in range(2):
                        sp.wait_ge(st_o[p], 16 * (NT // 2))

                @block.gpsimd
                def _(pool):
                    pool.iota(ie[:, :, :], pattern=[[0, NC], [-1, NE]], base=NE, channel_multiplier=0,
                              allow_small_or_imprecise_dtypes=True).then_inc(q_pool, 1)
                    pool.iota(tid[:, :, :], pattern=[[1, NTE + 1], [0, NE]], base=0, channel_multiplier=0,
                              allow_small_or_imprecise_dtypes=True).then_inc(q_pool, 1)
                    pool.memset(ones16[:, :], 1.0).then_inc(q_pool, 1)
                    pool.memset(below[:, :], 1.0).then_inc(q_pool, 1)
                    pool.wait_ge(q_pool, 4)
                    pool.affine_select(out=below[:, :], in_=below[:, :], compare_op=ALU.is_gt, fill=0.0,
                                       base=0, pattern=[[1, P]], channel_multiplier=-1).then_inc(q_pool, 1)

                    def put(b, first):
                        p = b.par()
                        if not first:
                            wait(pool, g_put[p], (b - 2).half(32 * PUT, 32 * PUT), alone)
                        pool.tensor_copy(idx[:, p, :, :], slot[:, bass.ds(b.index() * PUT, PUT), :]).then_inc(g_copy, 1)
                        pool.tensor_copy(ent[:, p], pair[:, bass.ds(b.index() * PUT, PUT)]).then_inc(g_copy, 1)
                        wait(pool, g_copy, b.count(2, 2), alone)
                        for t in range(PUT):
                            for c in range(2):
                                pool.indirect_dma_start(table, bass.IndirectOffsetOnAxis(idx[:, p, t, c:c + 1], 0),
                                                        ent[:, p, t, c, :], None).then_inc(g_put[p], 16)

                    pool.wait_ge(q_dve, ROUTED)
                    put(At(None, 0), True)
                    put(At(None, 1), True)
                    with pool.Fori(0, NC // PUT // 2 - 1) as it:
                        for u in range(2):
                            put(At(it, 2 + u), False)
                    for p in range(2):
                        pool.wait_ge(g_put[p], 32 * (NC // 2))

                @block.scalar
                def _(act):
                    def body(i, has):
                        if has(0):
                            for f in range(NF):
                                if is_body(i, 1) and f == 2:
                                    act.wait_ge(q_dve, 12)
                                    act.activation(ex[:, :], m[1][:, :], ACT.Exp).then_inc(q_act, 1)
                                wait(act, s_u, i.count(NF, f + 1))
                                wait(act, s_hlo, i.count(NF, f - 1))
                                act.activation(h32[:, f % 2], u_ps[f % 3][:, :], ACT.Gelu,
                                               scale=1.0 / WS).then_inc(s_h, 1)

                    bodies(act, body)

                @block.vector
                def _(dve):
                    dve.wait_ge(q_pool, 5)

                    steps = [0]

                    def step(ins, name=None):
                        steps[0] += 1
                        if name:
                            at[name] = steps[0]
                        ins.then_inc(q_dve, 1)
                        dve.wait_ge(q_dve, steps[0])

                    def over_e(v):
                        return v[:, :].unsqueeze(2).broadcast_to([P, NC, NE])

                    def largest(c):
                        src = l2 if c else lg
                        step(dve.tensor_reduce(m[c][:, :], src[:, :, :], AX_X, ALU.max))
                        step(dve.tensor_tensor(eq[:, :, :], src[:, :, :], over_e(m[c]), ALU.is_equal))
                        step(dve.tensor_tensor(eq[:, :, :], eq[:, :, :], ie[:, :, :], ALU.mult))

                    def chosen(c):
                        step(dve.tensor_reduce(sc[c][:, :], eq[:, :, :], AX_X, ALU.max))
                        step(dve.tensor_tensor(oh[c][:, :, :], ie[:, :, :], over_e(sc[c]), ALU.is_equal))
                        if c == 0:
                            step(dve.scalar_tensor_tensor(
                                l2[:, :, :].rearrange("p t e -> p (t e)"),
                                oh[0][:, :, :].rearrange("p t e -> p (t e)"), -3e38,
                                lg[:, :, :].rearrange("p t e -> p (t e)"), ALU.mult, ALU.add))
                        else:
                            step(dve.tensor_tensor(m[1][:, :], m[1][:, :], m[0][:, :], ALU.subtract), "diff")
                            step(dve.tensor_tensor(hot16[:, :, :], oh[0][:, :, :], oh[1][:, :, :], ALU.add), "hot")

                    def weights():
                        dve.wait_ge(q_act, 1)
                        step(dve.tensor_scalar(dn[:, :], ex[:, :], 1.0, None, ALU.add))
                        step(dve.reciprocal(w[0][:, :], dn[:, :]))
                        step(dve.tensor_tensor(w[1][:, :], w[0][:, :], ex[:, :], ALU.mult))
                        for c in range(2):
                            step(dve.tensor_scalar(pair[:, :, c, 1].bitcast(F32), w[c][:, :], tg[:, 0:1], 1.0 / WS,
                                                   ALU.mult, ALU.mult))

                    def totals():
                        dve.wait_ge(q_pe, 1)
                        step(dve.tensor_copy(tot[:, :, :].rearrange("p t e -> p (t e)"), z_ps[0][:, :]))

                    def prefix(k):
                        a, b, s = cum[1 - k % 2] if k else tot, cum[k % 2], 1 << k
                        step(dve.tensor_tensor(b[:, s:, :], a[:, s:, :], a[:, :NC - s, :], ALU.add))
                        step(dve.tensor_copy(b[:, :s, :], a[:, :s, :]))

                    assert NC == 1 << LEVELS
                    upto = cum[(LEVELS - 1) % 2]
                    ta = tiles[(NE.bit_length() - 2) % 2]

                    def expert_tiles():
                        step(dve.tensor_scalar(cnt[:, :], upto[:, NC - 1, :], float(TM - 1), None, ALU.add))
                        step(dve.tensor_copy(cnti[:, :], cnt[:, :]))
                        step(dve.tensor_scalar(cnti[:, :], cnti[:, :], TM.bit_length() - 1, None,
                                               ALU.arith_shift_right))
                        step(dve.tensor_copy(ntile[:, :], cnti[:, :]))
                        src, s = ntile, 1
                        while s < NE:
                            dst = tiles[1] if src is tiles[0] else tiles[0]
                            step(dve.tensor_tensor(dst[:, s:], src[:, s:], src[:, :NE - s], ALU.add))
                            step(dve.tensor_copy(dst[:, :s], src[:, :s]))
                            src, s = dst, s * 2
                        step(dve.tensor_tensor(tcmp[:, :, :], tid[:, :, :],
                                               ta[0:1, :].unsqueeze(1).broadcast_to([1, NTE + 1, NE]), ALU.is_ge))
                        step(dve.tensor_reduce(tef[:, :], tcmp[:, :, :], AX_X, ALU.add))
                        step(dve.tensor_scalar(tef[:, :], tef[:, :], float(NE - 1), None, ALU.min))
                        step(dve.tensor_copy(te[:, :], tef[:, :]))

                    def positions():
                        step(dve.tensor_tensor(cnt[:, :], ta[:, :], ntile[:, :], ALU.subtract))
                        step(dve.tensor_scalar(cnt[:, :], cnt[:, :], float(TM), None, ALU.mult))
                        step(dve.tensor_tensor(pos[:, :, :], upto[:, :, :], tot[:, :, :], ALU.subtract))
                        step(dve.tensor_tensor(pos[:, :, :], pos[:, :, :],
                                               cnt[:, :].unsqueeze(1).broadcast_to([P, NC, NE]), ALU.add))
                        step(dve.tensor_tensor(pos[:, :, :].rearrange("p t e -> p (t e)"),
                                               pos[:, :, :].rearrange("p t e -> p (t e)"), z_ps[1][:, :], ALU.add))

                    def slots(c):
                        step(dve.tensor_tensor(tmp[:, :, :], pos[:, :, :], oh[c][:, :, :], ALU.mult))
                        step(dve.tensor_reduce(sc[c][:, :], tmp[:, :, :], AX_X, ALU.add))
                        step(dve.tensor_copy(slot[:, :, c], sc[c][:, :]), "slots")

                    def route(tile, f):
                        k = tile * NF + f
                        if k in (0, 2):
                            largest(k // 2)
                        elif k in (1, 3):
                            chosen(k // 2)
                        elif k == 6:
                            weights()
                            totals()
                        elif 7 <= k < 7 + LEVELS // 2:
                            prefix(2 * (k - 7))
                            prefix(2 * (k - 7) + 1)
                        elif k == 7 + LEVELS // 2:
                            expert_tiles()
                            positions()
                        elif k == 8 + LEVELS // 2:
                            slots(0)
                            slots(1)

                    def body(i, has):
                        for f in range(NF):
                            if has(0):
                                n = i.count(NF, f + 1)
                                wait(dve, s_h, n)
                                if f == 0:
                                    wait(dve, s_d, (i - 2).count(2, 2))
                                dve.tensor_copy(hT[:, i.par(), HI, f], h32[:, f % 2]).then_inc(s_hhi, 1)
                                wait(dve, s_hhi, n)
                                dve.tensor_tensor(hT[:, i.par(), LO, f], h32[:, f % 2], hT[:, i.par(), HI, f],
                                                  ALU.subtract).then_inc(s_hlo, 1)
                            if f in (2, NF - 1) and has(-1):
                                b = i - 1
                                k = 0 if f == 2 else 1
                                wait(dve, s_d, b.count(2, k + 1))
                                wait(dve, l_r[b.par()], b.half(16, 16))
                                for t in (2 * k, 2 * k + 1):
                                    dve.scalar_tensor_tensor(xres[:, b.par(), t], d_ps[k][:, t % 2, :],
                                                             tgs[:, 0:1], xres[:, b.par(), t],
                                                             ALU.mult, ALU.add).then_inc(s_res, 1)
                            if i.it is None and i.c < PEEL:
                                route(i.c, f)

                    bodies(dve, body)

                @block.tensor
                def _(pe):
                    mm = nc.tensor.matmul
                    def body(i, has):
                        for f in range(NF):
                            if is_body(i, 1) and f == 2:
                                pe.wait_ge(q_pool, 5)
                                pe.wait_ge(q_dve, 13)
                                flat = hot16[:, :, :].rearrange("p t e -> p (t e)")
                                mm(z_ps[0][:, :], ones16[:, :], flat, start=True, stop=True)
                                mm(z_ps[1][:, :], below[:, :], flat, start=True, stop=True).then_inc(q_pe, 1)
                            if has(0):
                                wait(pe, s_h, i.count(NF, (0, -1, -1, 1)[f]))
                                n = 0
                                for k in range(DC):
                                    for pw, px in PASSES:
                                        ins = mm(u_ps[f % 3][:, :], s1[:, pw, k, f * P:(f + 1) * P],
                                                 xall[:, px, k, bass.ds(i.index() * TM, TM)],
                                                 start=(n == 0), stop=(n == 5))
                                        n += 1
                                ins.then_inc(s_u, 1)
                            if has(-1):
                                b = i - 1
                                if f == 0:
                                    wait(pe, s_hlo, b.count(NF, NF))
                                if f % 2 == 0:
                                    wait(pe, s_res, (b - 1).count(TQ, f + 2))
                                n = 0
                                for g in range(NF):
                                    for pw, px in PASSES:
                                        ins = mm(d_ps[f // 2][:, f % 2, :],
                                                 hT[:, b.par(), px, g, f * P:(f + 1) * P], s2[:, pw, g, :],
                                                 start=(n == 0), stop=(n == 3 * NF - 1))
                                        n += 1
                                if f % 2:
                                    ins.then_inc(s_d, 1)

                    bodies(pe, body)

            assert at == {"diff": 12, "hot": 13, "slots": ROUTED}
        early.close()

        with ExitStack() as c4:
            tab = sb("tab", [P, 2, TQ, 2], I32, c4)
            tab2 = sb("tab2", [P, 2, TQ, 2], I32, c4)
            gix = sb("gix", [P, 2, TQ], I32, c4)
            xg = sb("xg", [P, 2, TQ, D], F32, c4)
            xT = sb("exT", [P, 2, 2, DC, TM], F16, c4)
            h32 = sb("eh32", [P, 2, TM], F32, c4)
            hT = sb("ehT", [P, 2, 2, NF, TM], F16, c4)
            y = sb("y", [P, 2, TQ, D], F32, c4)
            t_ps = [pb(f"et_ps{k}", [P, TM], F32, c4) for k in range(DC)]
            u_ps = [pb(f"eu_ps{i}", [P, TM], F32, c4) for i in range(3)]
            d_ps = [pb(f"ed_ps{i}", [P, 2, D], F32, c4) for i in range(2)]
            l_t = [sem(f"e_lt{i}") for i in range(2)]
            l_t2 = [sem(f"e_ltt{i}") for i in range(2)]
            g_x = [sem(f"e_gx{i}") for i in range(2)]
            g_y = [sem(f"e_gy{i}") for i in range(2)]
            s_ix = sem("e_ix")
            s_xt = sem("e_xt")
            s_xhi = sem("e_xhi")
            s_xlo = sem("e_xlo")
            s_u = sem("e_u")
            s_h = sem("e_h")
            s_hhi = sem("e_hhi")
            s_hlo = sem("e_hlo")
            s_d = sem("e_d")
            s_y = sem("e_y")

            def bodies(eng, body):
                loop_bodies(eng, body, -2, 3, NTE - 2, NTE)

            assert NTE % 2
            AT = dict(x=1, hi=1, lo=1, y0=2, y1=3)

            with nc.Block() as block:
                @block.sync
                def _(sp):
                    def body(i, has):
                        if has(2):
                            b = i + 2
                            wait(sp, s_ix, (b - 2).count(1, 1), alone)
                            sp.dma_start(tab[:, b.par()], table_t[b.index()]).then_inc(l_t[b.par()], 16)
                        if has(0):
                            wait(sp, g_y[i.par()], (i - 2).half(16 * TQ, 16 * TQ), alone)
                            sp.dma_start(tab2[:, i.par()], table_t[i.index()]).then_inc(l_t2[i.par()], 16)

                    bodies(sp, body)

                @block.gpsimd
                def _(pool):
                    def body(i, has):
                        if has(2):
                            b = i + 2
                            p = b.par()
                            wait(pool, s_ix, b.count(1, 1), alone)
                            wait(pool, s_xt, (b - 2).count(DC, DC), alone)
                            for t in range(TQ):
                                pool.indirect_dma_start(xg[:, p, t], None, xn_d,
                                                        bass.IndirectOffsetOnAxis(gix[:, p, t:t + 1], 0))\
                                    .then_inc(g_x[p], 16)
                        if has(-1):
                            b = i - 1
                            p = b.par()
                            wait(pool, s_y, b.count(TQ, TQ), alone)
                            wait(pool, g_y[1 - p], (b - 1).half(16 * TQ, 16 * TQ), alone)
                            for t in range(TQ):
                                pool.indirect_dma_start(out, bass.IndirectOffsetOnAxis(tab2[:, p, t, 0:1], 0),
                                                        y[:, p, t], None, bounds_check=T - 1, oob_is_err=False,
                                                        compute_op=ALU.add).then_inc(g_y[p], 16)

                    bodies(pool, body)
                    pool.wait_ge(g_y[0], 16 * TQ * ((NTE + 1) // 2))
                    pool.wait_ge(g_y[1], 16 * TQ * (NTE // 2))

                @block.scalar
                def _(act):
                    def body(i, has):
                        for f in range(NF):
                            if has(0):
                                wait(act, s_u, i.count(NF, f + 1))
                                wait(act, s_hlo, i.count(NF, f - 1))
                                act.activation(h32[:, f % 2], u_ps[f % 3][:, :], ACT.Gelu,
                                               scale=1.0 / WS).then_inc(s_h, 1)
                            if f == AT['hi'] and has(1):
                                b = i + 1
                                wait(act, s_u, (b - 2).count(NF, NF))
                                for k in range(DC):
                                    wait(act, s_xt, b.count(DC, k + 1))
                                    act.activation(xT[:, b.par(), HI, k], t_ps[k][:, :],
                                                   ACT.Identity).then_inc(s_xhi, 1)

                    bodies(act, body)

                @block.vector
                def _(dve):
                    def body(i, has):
                        def results(k):
                            b = i - 1
                            p = b.par()
                            wait(dve, s_d, b.count(2, k + 1))
                            if k == 0:
                                wait(dve, l_t2[p], b.half(16, 16))
                                wait(dve, g_y[p], (b - 2).half(16 * TQ, 16 * TQ))
                            for t in (2 * k, 2 * k + 1):
                                dve.tensor_scalar(y[:, p, t], d_ps[k][:, t % 2, :],
                                                  tab2[:, p, t, 1:2].bitcast(F32), None,
                                                  ALU.mult).then_inc(s_y, 1)

                        if has(2):
                            b = i + 2
                            p = b.par()
                            wait(dve, l_t[p], b.half(16, 16))
                            wait(dve, g_x[p], (b - 2).half(16 * TQ, 16 * TQ))
                            dve.tensor_scalar(gix[:, p], tab[:, p, :, 0], T - 1, None,
                                              ALU.min).then_inc(s_ix, 1)
                        for f in range(NF):
                            if has(0):
                                n = i.count(NF, f + 1)
                                wait(dve, s_h, n)
                                if f == 0:
                                    wait(dve, s_d, (i - 2).count(2, 2))
                                dve.tensor_copy(hT[:, i.par(), HI, f], h32[:, f % 2]).then_inc(s_hhi, 1)
                                wait(dve, s_hhi, n)
                                dve.tensor_tensor(hT[:, i.par(), LO, f], h32[:, f % 2], hT[:, i.par(), HI, f],
                                                  ALU.subtract).then_inc(s_hlo, 1)
                            if f == AT['lo'] and has(1):
                                b = i + 1
                                for k in range(DC):
                                    wait(dve, s_xhi, b.count(DC, k + 1))
                                    dve.tensor_tensor(xT[:, b.par(), LO, k], t_ps[k][:, :], xT[:, b.par(), HI, k],
                                                      ALU.subtract).then_inc(s_xlo, 1)
                            if f in (AT['y0'], AT['y1']) and has(-1):
                                results(0 if f == AT['y0'] else 1)

                    bodies(dve, body)

                @block.tensor
                def _(pe):
                    mm = nc.tensor.matmul

                    def body(i, has):
                        if has(0):
                            e = pe.value_load(te[0:1, bass.ds(i.index(), 1)], min_val=0, max_val=NE - 1)
                        if has(-1):
                            e_d = pe.value_load(te[0:1, bass.ds((i - 1).index(), 1)], min_val=0, max_val=NE - 1)
                        for f in range(NF):
                            if has(0):
                                if f == 0:
                                    wait(pe, s_xlo, i.count(DC, DC))
                                wait(pe, s_h, i.count(NF, (0, -1, -1, 1)[f]))
                                n = 0
                                for k in range(DC):
                                    for pw, px in PASSES:
                                        ins = mm(u_ps[f % 3][:, :], wu_all[:, pw, bass.ds(e * WN + (k * FE + f * P), P)],
                                                 xT[:, i.par(), px, k, :], start=(n == 0), stop=(n == 5))
                                        n += 1
                                ins.then_inc(s_u, 1)
                            if has(-1):
                                b = i - 1
                                if f == 0:
                                    wait(pe, s_hlo, b.count(NF, NF))
                                if f % 2 == 0:
                                    wait(pe, s_y, (b - 1).count(TQ, f + 2))
                                n = 0
                                for g in range(NF):
                                    for pw, px in PASSES:
                                        ins = mm(d_ps[f // 2][:, f % 2, :],
                                                 hT[:, b.par(), px, g, f * P:(f + 1) * P],
                                                 wd_all[:, pw, bass.ds(e_d * WN + g * D, D)], start=(n == 0), stop=(n == 3 * NF - 1))
                                        n += 1
                                if f % 2:
                                    ins.then_inc(s_d, 1)
                            if f == AT['x'] and has(1):
                                b = i + 1
                                wait(pe, g_x[b.par()], b.half(16 * TQ, 16 * TQ))
                                wait(pe, s_xlo, (b - 1).count(DC, DC))
                                for k in range(DC):
                                    for t in range(TQ):
                                        ins = pe.transpose(t_ps[k][:, t * P:(t + 1) * P],
                                                           xg[:, b.par(), t, k * P:(k + 1) * P], ident[:, :])
                                    ins.then_inc(s_xt, 1)

                    bodies(pe, body)

        clear(nc, sems)


def gated_transformer(nc, a, out):
    T = a["x"].shape[0]
    NB = T // S
    x1 = nc.dram_tensor("x1", (T, D), F32, kind="Internal").ap()
    x2 = nc.dram_tensor("x2", (T, D), F32, kind="Internal").ap()
    x3 = nc.dram_tensor("x3", (T, D), F32, kind="Internal").ap()
    attention(nc, "a0", NB, a["x"], a["ctxT"], a["L0_WqT"], a["L0_WkT"], a["L0_WvT"], a["L0_WoT"], None,
              a["g_xattn"][0:1], x1)
    ternary_mlp(nc, "f0", T // TM, x1, a["L0_w_upT"], a["L0_w_downT"], a["g_ffn"][0:1], x2)
    attention(nc, "a1", NB, x2, a["ctxT"], a["L1_Wq"], a["L1_Wk"], a["L1_Wv"], a["L1_Wo"],
              (a["L1_bqT"], a["L1_bkT"], a["L1_bv"], a["L1_bo"]), a["g_xattn"][1:2], x3)
    moe(nc, "m1", T // TM, x3, a["L1_Wg"], a["L1_Wu"], a["L1_Wd"], a["L1_W1"], a["L1_W2"], a["g_ffn"][1:2], out)


def kernel(**inputs):
    import numpy as _np
    import concourse.bacc as _bacc
    from concourse import mybir as _mybir
    from concourse.bass_utils import run_bass_kernel_spmd as _run

    v = {n: _np.asarray(x) for n, x in inputs.items()}
    shape = v["x"].shape
    tokens = shape[0] * shape[1]
    laid = {
        "x": v["x"].reshape(tokens, D),
        "ctxT": v["ctx_1024"].reshape(tokens, D).T,
        "g_xattn": v["g_xattn"],
        "g_ffn": v["g_ffn"],
        "L0_WqT": v["L0_xattn_Wq"].T,
        "L0_WkT": v["L0_xattn_Wk"].T,
        "L0_WvT": v["L0_xattn_Wv"].T,
        "L0_WoT": v["L0_xattn_Wo"].T,
        "L0_w_upT": v["L0_ffn_w_up"].T,
        "L0_w_downT": v["L0_ffn_w_down"].T,
        "L1_Wq": v["L1_xattn_Wq"],
        "L1_Wk": v["L1_xattn_Wk"],
        "L1_Wv": v["L1_xattn_Wv"],
        "L1_Wo": v["L1_xattn_Wo"],
        "L1_bqT": v["L1_xattn_bq"].reshape(DC, P).T,
        "L1_bkT": v["L1_xattn_bk"].reshape(DC, P).T,
        "L1_bv": v["L1_xattn_bv"],
        "L1_bo": v["L1_xattn_bo"],
        "L1_Wg": v["L1_ffn_Wg"],
        "L1_Wu": v["L1_ffn_Wu"],
        "L1_Wd": v["L1_ffn_Wd"],
        "L1_W1": v["L1_ffn_W1"],
        "L1_W2": v["L1_ffn_W2"],
    }
    nc = _bacc.Bacc("TRN2", target_bir_lowering=False, num_devices=1)
    arrays, args = {}, {}
    for name, value in laid.items():
        value = _np.ascontiguousarray(value)
        arrays[f"in_{name}"] = value
        args[name] = nc.dram_tensor(f"in_{name}", value.shape, _mybir.dt.from_np(value.dtype),
                                    kind="ExternalInput").ap()
    out = nc.dram_tensor("out_0", (tokens, D), F32, kind="ExternalOutput").ap()
    gated_transformer(nc, args, out)
    r = _run(nc, [arrays], core_ids=[0])
    return _np.asarray(r.results[0]["out_0"]).reshape(shape)
```
